# Optimizing a Trainium2 kernel written in Bass

```python
import numpy as np
import jax
import jax.numpy as jnp

def _softmax(x, axis=-1):
    return jax.nn.softmax(x, axis=axis)

def _gelu(x):
    return jax.nn.gelu(x, approximate=True)

def _silu(x):
    return jax.nn.silu(x)

def _sigmoid(x):
    return jax.nn.sigmoid(x)

def _layernorm(x, axis=-1, eps=1e-05):
    m = jnp.mean(x, axis=axis, keepdims=True)
    v = jnp.var(x, axis=axis, keepdims=True)
    return (x - m) / jnp.sqrt(v + eps)

def _scatter_add(tgt, idx, src, axis=0):
    return tgt.at[idx].add(src)

def _segment_sum(src, seg, n):
    return jax.ops.segment_sum(src, seg, n)
kernel_name = 'mk_xattn_ffn_d1_seqx_r4_ef2cb3'

def setup_inputs(seed: int=0):
    np.random.seed(seed)
    _w = jnp.asarray

    def _rec_inputs():
        import jax
        import jax.numpy as jnp
        _rk = jax.random.key(seed)
        x = -0.0002928 + 1 * jax.random.normal(jax.random.fold_in(_rk, 1), (16, 256, 512), jnp.float32)
        _lenS = 256 - jax.random.randint(jax.random.fold_in(_rk, 7), (16,), 0, max(1, 256 // 4) + 1, jnp.int32)
        _lenS2 = 256 - jax.random.randint(jax.random.fold_in(_rk, 8), (16,), 0, max(1, 256 // 4) + 1, jnp.int32)
        fside_S2_0 = -0.00337071 + 1.01897 * jax.random.normal(jax.random.fold_in(_rk, 11), (256,), jnp.float32)
        _ctx_2048P = jax.random.normal(jax.random.fold_in(_rk, 12), (16, 16, 512), jnp.float32)
        _ctx_2048c = jax.random.dirichlet(jax.random.fold_in(_rk, 512), 0.3 * jnp.ones((16,), jnp.float32), (16, 256))
        _ctx_2048t = jnp.einsum('bsk,bkd->bsd', _ctx_2048c, _ctx_2048P)
        _ctx_2048t = _ctx_2048t * jax.lax.rsqrt(jnp.mean(jnp.square(_ctx_2048t)) + 1e-12) * 0.953939
        ctx_2048 = 0.000675642 + 1.00031 * (_ctx_2048t + 0.3 * jax.random.normal(jax.random.fold_in(_rk, 612), (16, 256, 512), jnp.float32))
        return (x, fside_S2_0, ctx_2048)
    x, fside_S2_0, ctx_2048 = _rec_inputs()

    def _L0_xattn_setup():
        import jax, jax.numpy as jnp
        import numpy as np
        key = jax.random.key(seed)
        ks = jax.random.split(key, 5)
        B, D, L, NH = (2, 256, 512, 8)
        H = D // NH
        return {'v': jax.random.normal(ks[0], (B, D, L), jnp.float32), 'k': jax.random.normal(ks[1], (H, L), jnp.float32) * 0.1, 'bias': jax.random.normal(ks[2], (D,), jnp.float32), 'x1': jax.random.normal(ks[3], (B, D, L), jnp.float32), 'x2': jax.random.normal(ks[4], (B, D, L), jnp.float32), 'num_heads': NH}
    _L0_xattn_all = _L0_xattn_setup()
    _L0_xattn_in = {k: v for k, v in _L0_xattn_all.items() if k in ('k',)}
    del _L0_xattn_all

    def _L0_ffn_setup():
        import jax, jax.numpy as jnp
        import numpy as np
        E = 64
        K = 6
        CAP = 128
        SCALE = 1.0
        H = 512
        I = 192
        SI = I * 2
        B, S = (2, 256)

        def _moe(x, gate_w, gate_up_proj, down_proj, shared_gate_w, shared_up_w, shared_down_w):
            b, s, h = x.shape
            T = b * s
            xf = x.reshape(T, h)
            scores = jax.nn.softmax(xf @ gate_w.T, axis=-1)
            topk_w, topk_idx = jax.lax.top_k(scores, K)
            topk_w = topk_w * SCALE
            flat_e = topk_idx.reshape(-1)
            order = jnp.argsort(flat_e)
            sorted_e = flat_e[order]
            sorted_tok = (order // K).astype(jnp.int32)
            sorted_w = topk_w.reshape(-1)[order]
            counts = jnp.zeros((E,), jnp.int32).at[flat_e].add(1)
            offsets = jnp.cumsum(counts) - counts
            pos = jnp.arange(T * K, dtype=jnp.int32) - offsets[sorted_e]
            buf_tok = jnp.full((E, CAP), T, jnp.int32).at[sorted_e, pos].set(sorted_tok, mode='drop')
            buf_w = jnp.zeros((E, CAP), x.dtype).at[sorted_e, pos].set(sorted_w, mode='drop')
            xp = jnp.concatenate([xf, jnp.zeros((1, h), x.dtype)], axis=0)
            gx = xp[buf_tok]
            gu = jnp.einsum('ech,ehi->eci', gx, gate_up_proj)
            g, u = jnp.split(gu, 2, axis=-1)
            hid = jax.nn.silu(g) * u
            eo = jnp.einsum('eci,eih->ech', hid, down_proj) * buf_w[..., None]
            routed = jnp.zeros((T + 1, h), x.dtype).at[buf_tok.reshape(-1)].add(eo.reshape(-1, h))[:T]
            shared = jax.nn.silu(xf @ shared_gate_w.T) * (xf @ shared_up_w.T) @ shared_down_w.T
            return (routed + shared).reshape(b, s, h)
        key = jax.random.key(seed)
        ks = jax.random.split(key, 7)
        x = jax.random.normal(ks[0], (B, S, H), jnp.float32)
        gate_w = jax.random.normal(ks[1], (E, H), jnp.float32) * 0.02
        gate_up_proj = jax.random.normal(ks[2], (E, H, 2 * I), jnp.float32) * 0.02
        down_proj = jax.random.normal(ks[3], (E, I, H), jnp.float32) * 0.02
        shared_gate_w = jax.random.normal(ks[4], (SI, H), jnp.float32) * 0.02
        shared_up_w = jax.random.normal(ks[5], (SI, H), jnp.float32) * 0.02
        shared_down_w = jax.random.normal(ks[6], (H, SI), jnp.float32) * 0.02
        return dict(x=x, gate_w=gate_w, gate_up_proj=gate_up_proj, down_proj=down_proj, shared_gate_w=shared_gate_w, shared_up_w=shared_up_w, shared_down_w=shared_down_w)
    _L0_ffn_all = _L0_ffn_setup()
    _L0_ffn_in = {k: v for k, v in _L0_ffn_all.items() if k in ('gate_w', 'gate_up_proj', 'down_proj', 'shared_gate_w', 'shared_up_w', 'shared_down_w')}
    del _L0_ffn_all
    return {'x': x, 'fside_S2_0': fside_S2_0, 'ctx_2048': ctx_2048, 'L0_xattn_k': _L0_xattn_in['k'], 'L0_ffn_gate_w': _L0_ffn_in['gate_w'], 'L0_ffn_gate_up_proj': _L0_ffn_in['gate_up_proj'], 'L0_ffn_down_proj': _L0_ffn_in['down_proj'], 'L0_ffn_shared_gate_w': _L0_ffn_in['shared_gate_w'], 'L0_ffn_shared_up_w': _L0_ffn_in['shared_up_w'], 'L0_ffn_shared_down_w': _L0_ffn_in['shared_down_w']}

def reference(x, fside_S2_0, ctx_2048, L0_xattn_k, L0_ffn_gate_w, L0_ffn_gate_up_proj, L0_ffn_down_proj, L0_ffn_shared_gate_w, L0_ffn_shared_up_w, L0_ffn_shared_down_w):
    import jax
    import jax.numpy as jnp

    def _L0_xattn_ref(v, k, bias, x1, x2, num_heads):
        import jax, jax.numpy as jnp
        import numpy as np
        B, D, L = v.shape
        H = D // num_heads
        fft_size = 2 * L
        vr = v.reshape(B, H, num_heads, L)
        x1r = x1.reshape(B, H, num_heads, L)
        x2r = x2.reshape(B, H, num_heads, L)
        kv = vr[:, :, :, None, :] * x2r[:, :, None, :, :]
        k_f = jnp.fft.rfft(k.astype(jnp.float32), n=fft_size)
        y = jnp.fft.irfft(jnp.fft.rfft(kv, n=fft_size) * k_f[None, :, None, None, :], n=fft_size)[..., :L]
        skip = bias.astype(jnp.float32).reshape(H, num_heads)[None, :, :, None, None]
        y = y + kv * skip
        out = jnp.einsum('bhijl,bhil->bhjl', y, x1r)
        return out.reshape(B, D, L)

    def _L0_ffn_ref(x, gate_w, gate_up_proj, down_proj, shared_gate_w, shared_up_w, shared_down_w):
        import jax, jax.numpy as jnp
        import numpy as np
        E = 64
        K = 6
        CAP = 128
        SCALE = 1.0
        H = 512
        I = 192
        SI = I * 2
        B, S = (2, 256)

        def _moe(x, gate_w, gate_up_proj, down_proj, shared_gate_w, shared_up_w, shared_down_w):
            b, s, h = x.shape
            T = b * s
            xf = x.reshape(T, h)
            scores = jax.nn.softmax(xf @ gate_w.T, axis=-1)
            topk_w, topk_idx = jax.lax.top_k(scores, K)
            topk_w = topk_w * SCALE
            flat_e = topk_idx.reshape(-1)
            order = jnp.argsort(flat_e)
            sorted_e = flat_e[order]
            sorted_tok = (order // K).astype(jnp.int32)
            sorted_w = topk_w.reshape(-1)[order]
            counts = jnp.zeros((E,), jnp.int32).at[flat_e].add(1)
            offsets = jnp.cumsum(counts) - counts
            pos = jnp.arange(T * K, dtype=jnp.int32) - offsets[sorted_e]
            buf_tok = jnp.full((E, CAP), T, jnp.int32).at[sorted_e, pos].set(sorted_tok, mode='drop')
            buf_w = jnp.zeros((E, CAP), x.dtype).at[sorted_e, pos].set(sorted_w, mode='drop')
            xp = jnp.concatenate([xf, jnp.zeros((1, h), x.dtype)], axis=0)
            gx = xp[buf_tok]
            gu = jnp.einsum('ech,ehi->eci', gx, gate_up_proj)
            g, u = jnp.split(gu, 2, axis=-1)
            hid = jax.nn.silu(g) * u
            eo = jnp.einsum('eci,eih->ech', hid, down_proj) * buf_w[..., None]
            routed = jnp.zeros((T + 1, h), x.dtype).at[buf_tok.reshape(-1)].add(eo.reshape(-1, h))[:T]
            shared = jax.nn.silu(xf @ shared_gate_w.T) * (xf @ shared_up_w.T) @ shared_down_w.T
            return (routed + shared).reshape(b, s, h)
        return _moe(x, gate_w, gate_up_proj, down_proj, shared_gate_w, shared_up_w, shared_down_w)
    x = x + _L0_xattn_ref(_layernorm(x, axis=-1), L0_xattn_k, fside_S2_0, ctx_2048, ctx_2048, 8)
    x = x + _L0_ffn_ref(_layernorm(x, axis=-1), L0_ffn_gate_w, L0_ffn_gate_up_proj, L0_ffn_down_proj, L0_ffn_shared_gate_w, L0_ffn_shared_up_w, L0_ffn_shared_down_w)
    return x

_drawn_inputs = setup_inputs


def setup_inputs(seed=0):
    import zlib

    import numpy as np

    out = dict(_drawn_inputs(seed))
    spreads = {}
    factors = {'L0_ffn_gate_w': 8.0,
     'L0_ffn_gate_up_proj': 8.0,
     'L0_ffn_down_proj': 8.0,
     'L0_ffn_shared_gate_w': 7.87,
     'L0_ffn_shared_up_w': 7.671,
     'L0_ffn_shared_down_w': 7.672}
    for name, (base, spread) in spreads.items():
        noise = np.random.default_rng([zlib.crc32(name.encode()), seed]).standard_normal(out[name].shape)
        drawn = base * np.exp(spread * noise) if base else spread * noise
        out[name] = jnp.asarray(drawn.astype(out[name].dtype))
    for name, factor in factors.items():
        out[name] = (out[name] * factor).astype(out[name].dtype)
    return out
```

```python
from contextlib import ExitStack

import numpy as np

import concourse.bass as bass
from concourse import mybir

F32 = mybir.dt.float32
BF16 = mybir.dt.bfloat16
I32 = mybir.dt.int32
U32 = mybir.dt.uint32
ALU = mybir.AluOpType
ACT = mybir.ActivationFunctionType
AX = mybir.AxisListType

P = 128
B, D, L = 16, 256, 512
NH = 8
NT = D // NH
T = B * D
NC = L // P
E, K, CAP = 64, 6, 128
I = 192
SI = 2 * I
IH = I // 2
EPS = 1e-5
FLOOR = -87.3
NW = 4


def build(nc, x, skip, ctx_in, k, gate_w, gate_up, down, sh_gate, sh_up, sh_down,
          c_sq, c_iota, c_rec, c_table, out):
    xn_rows = nc.dram_tensor("xn_rows", [T + CAP, L], F32, kind="Internal").ap()
    x1_rows = nc.dram_tensor("x1_rows", [T, L], F32, kind="Internal").ap()
    krev = nc.dram_tensor("krev", [NT, L + P], F32, kind="Internal").ap()
    table = nc.dram_tensor("table", [CAP * E, 2], F32, kind="Internal").ap()

    with ExitStack() as stack:
        def sb(name, shape, dt=F32):
            return stack.enter_context(nc.sbuf_tensor(name, shape, dt))

        def ps(name):
            return stack.enter_context(nc.psum_tensor(name, [P, 512], F32))

        def sem(name):
            return stack.enter_context(nc.semaphore(name))

        sq = sb("sq", [P, 5, P])
        ident, same_b = sq[:, 0, :], sq[:, 1, :]
        sq16 = sb("sq16", [P, 3, P], BF16)
        iota = sb("iota", [P, E])
        eps = sb("eps", [P, 1])
        zeros = sb("zeros", [P, L])
        kpad = sb("kpad", [NT, L + P])
        gate_in = sb("gate_in", [E, L])
        gateT = sb("gateT", [P, NC, E])
        sh_guT = sb("sh_guT", [P, NC, 2 * SI])
        sh_dT = sb("sh_dT", [P, SI // P, L])
        ring = sb("ring", [P, NW, NC * SI + 2 * L])
        xt = sb("xt", [P, 2, L])
        ct = sb("ct", [P, 2, L])
        gr = sb("gr", [P, 2, L])
        toep = sb("toep", [P, 2, L])
        skip_c = sb("skip_c", [P, 2, 1])
        v = sb("v", [P, 2, L])
        w = sb("w", [P, 2, L])
        vT = sb("vT", [P, 2, NC, P])
        cT = sb("cT", [P, 2, NC, P])
        kv = sb("kv", [P, 2, NC, B * NH * NH])
        z = sb("z", [P, 4, 512])
        kin = z[0:NT, 0, :]
        o = sb("o", [P, 2, NC, P])
        xr = sb("xr", [P, 2, L])
        x1 = sb("x1", [P, 2, L])
        xn = sb("xn", [P, 2, L])
        xT = sb("xT", [P, 2, NC, P])
        st1, mv1, sd1, rs1 = sb("st1", [P, 6]), sb("mv1", [P, 2]), sb("sd1", [P, 1]), sb("rs1", [P, 1])
        st2, mv2, sd2, rs2 = sb("st2", [P, 6]), sb("mv2", [P, 2]), sb("sd2", [P, 1]), sb("rs2", [P, 1])
        m8 = sb("m8", [P, 8])
        sc = sb("sc", [P, E])
        s8 = sb("s8", [P, 8])
        i8 = sb("i8", [P, 8], U32)
        sc_all = sb("sc_all", [P, NT, E])
        s8_all = sb("s8_all", [P, NT, 8])
        idx_all = sb("idx_all", [P, NT, K])
        onehot = sb("onehot", [P, NT, K, E], BF16)
        mask = sb("mask", [P, NT, E], BF16)
        pre = sb("pre", [P, NT + 1, E], BF16)
        sums, rinv = sb("sums", [P, NT]), sb("rinv", [P, NT])
        rec = sb("rec", [P, NT, K, 2])
        pk = sb("pk", [P, K])
        slot = sb("slot", [P, 2, K], I32)
        recs = sb("recs", [P, 2, K, 2])
        tbl = sb("tbl", [P, E, 2])
        idx_i = sb("idx_i", [P, E], I32)
        idx4 = sb("idx4", [P, 4], I32)
        sg = kv[:, 0, 0:1, 0:2 * SI].rearrange("p a (s n) -> p (a s) n", s=2)
        hid = kv[:, 0, 1:2, 0:2 * SI].rearrange("p a (s n) -> p (a s) n", s=2)
        hT = kv[:, 0, 2:3, 0:2 * SI].rearrange("p a (s c n) -> p (a s) c n", s=2, c=3)
        y = kv[:, 1, 0:1, :].rearrange("p a (s n) -> p (a s) n", s=2)
        prod = kv[:, 0, 3:4, 0:K * E].rearrange("p a (k e) -> p (a k) e", e=E)
        pos = kv[:, 1, 2:4, :].rearrange("p a (t e) -> p (a t) e", e=E)
        xg = kv[:, 1, 1:2, :].rearrange("p a (s n) -> p (a s) n", s=2)

        Y = [ps(f"Y{n}") for n in range(4)]
        TA, TB, OT, DX = ps("TA"), ps("TB"), ps("OT"), ps("DX")
        DN = [OT, DX]

        consts_in, small_in = sem("consts_in"), sem("small_in")
        gate_w_in, sh_gu_in, sh_down_in = sem("gate_w_in"), sem("sh_gu_in"), sem("sh_down_in")
        dve_setup, krev_ready, krev_out, pads_out = sem("dve_setup"), sem("krev_ready"), sem("krev_out"), sem("pads_out")
        dve_turn, pool_turn = sem("dve_turn"), sem("pool_turn")
        w_ps, w_sb = sem("w_ps"), sem("w_sb")
        tile_in = [sem("tile_in0"), sem("tile_in1")]
        ln1_stats, ln1_mv, ln1_sd, ln1_rstd = sem("ln1_stats"), sem("ln1_mv"), sem("ln1_sd"), sem("ln1_rstd")
        v_ready, w_ready, g_ready = sem("v_ready"), sem("w_ready"), sem("g_ready")
        vT_ps, cT_ps, dx_ps, vT_sb, cT_sb = sem("vT_ps"), sem("cT_ps"), sem("dx_ps"), sem("vT_sb"), sem("cT_sb")
        kv_ready, conv_done, z_done, o_done = sem("kv_ready"), sem("conv_done"), sem("z_done"), sem("o_done")
        dc_ready, xr_ready, oT_ps, x1_ready = sem("dc_ready"), sem("xr_ready"), sem("oT_ps"), sem("x1_ready")
        ln2_stats, ln2_mv, ln2_sd, ln2_rstd = sem("ln2_stats"), sem("ln2_mv"), sem("ln2_sd"), sem("ln2_rstd")
        xn_ready, xT_ps, xT_sb, logit_ps = sem("xn_ready"), sem("xT_ps"), sem("xT_sb"), sem("logit_ps")
        x1_out, xn_out = [sem("x1_out0"), sem("x1_out1")], [sem("xn_out0"), sem("xn_out1")]
        max_ready, sc_ready, s8_ready, i8_ready = sem("max_ready"), sem("sc_ready"), sem("s8_ready"), sem("i8_ready")
        sc_kept, idx_ready, onehot_ready = sem("sc_kept"), sem("idx_ready"), sem("onehot_ready")
        mask_ready, pre_ready = sem("mask_ready"), sem("pre_ready")
        pos_ps, pos_sb, exp_ready = sem("pos_ps"), sem("pos_sb"), sem("exp_ready")
        sums_ready, rinv_ready, rec_ready = sem("sums_ready"), sem("rinv_ready"), sem("rec_ready")
        prod_ready, pk_ready, slot_ready = sem("prod_ready"), sem("pk_ready"), sem("slot_ready")
        placed = [sem("placed0"), sem("placed1")]
        b_xn_in, b_x1_in = [sem("b_xn_in0"), sem("b_xn_in1")], [sem("b_x1_in0"), sem("b_x1_in1")]
        b_xT_ps, b_xT_sb, gate_ps, up_ps = sem("b_xT_ps"), sem("b_xT_sb"), sem("gate_ps"), sem("up_ps")
        b_silu, b_hid, b_hT_ps, b_hT_sb, b_down = sem("b_silu"), sem("b_hid"), sem("b_hT_ps"), sem("b_hT_sb"), sem("b_down")
        y_ready, y_out = sem("y_ready"), [sem("y_out0"), sem("y_out1")]
        table_in, idx_i_ready, idx4_ready = sem("table_in"), sem("idx_i_ready"), sem("idx4_ready")
        weights_in = [sem(f"weights_in{r}") for r in range(NW)]
        gathered = [sem("gathered0"), sem("gathered1")]
        c_xT_ps, c_xT_sb, c_gu, c_silu = sem("c_xT_ps"), sem("c_xT_sb"), sem("c_gu"), sem("c_silu")
        c_hid, c_hT_ps, c_hT_sb, c_down = sem("c_hid"), sem("c_hT_ps"), sem("c_hT_sb"), sem("c_down")
        eo_ready, added = sem("eo_ready"), sem("added")

        def rows(dram, h):
            return dram.rearrange("(b h i) l -> h b i l", b=B, i=NH)[h]

        def landed(n, s, each):
            return (n - s) * (each // 2) + each

        def among(n, *numbers):
            return isinstance(n, int) and n in numbers

        x_f = x.rearrange("b d l -> (b d) l")
        c_f = ctx_in.rearrange("b d l -> (b d) l")
        skip_v = skip.rearrange("(h i) -> h i", i=NH)
        n_up = SI // P

        def weights(sp, e, r):
            sp.dma_start(ring[:, r, 0:NC * SI].rearrange("p (c n) -> p c n", c=NC),
                         gate_up[e].rearrange("(c p) n -> p c n", p=P)).then_inc(weights_in[r], 16)
            sp.dma_start(ring[0:IH, r, NC * SI:].rearrange("p (c n) -> p c n", c=2),
                         down[e].rearrange("(c p) n -> p c n", p=IH)).then_inc(weights_in[r], 16)

        block = stack.enter_context(nc.Block())

        @block.sync
        def _(sp):
            sp.dma_start(kin, k).then_inc(small_in, 16)
            sp.dma_start(sq[:, 0:4, :], c_sq).then_inc(consts_in, 16)
            sp.dma_start(gate_in[:], gate_w).then_inc(gate_w_in, 16)
            sp.dma_start(ring[:, 0, 0:n_up * L].rearrange("p (a l) -> p a l", a=n_up),
                         sh_gate.rearrange("(a p) l -> p a l", p=P)).then_inc(sh_gu_in, 16)
            sp.dma_start(ring[:, 1, 0:n_up * L].rearrange("p (a l) -> p a l", a=n_up),
                         sh_up.rearrange("(a p) l -> p a l", p=P)).then_inc(sh_gu_in, 16)
            sp.dma_start(ring[:, 2, 0:NC * SI].rearrange("p (a i) -> p a i", a=NC),
                         sh_down.rearrange("(a p) i -> p a i", p=P)).then_inc(sh_down_in, 16)
            sp.dma_start(iota[:], c_iota).then_inc(small_in, 16)
            sp.dma_start(rec[:].rearrange("p t k c -> p (t k c)"), c_rec).then_inc(small_in, 16)
            sp.wait_ge(dve_setup, 3)
            sp.wait_ge(krev_ready, 1)
            sp.dma_start(krev, kpad[:]).then_inc(krev_out, 16)
            sp.dma_start(table, c_table).then_inc(pads_out, 16)
            sp.dma_start(xn_rows[T:T + CAP, :], zeros[:]).then_inc(pads_out, 16)
            sp.dma_start(out[T:T + CAP, :], zeros[:]).then_inc(pads_out, 16)
            sp.wait_ge(krev_out, 16)

            def load(h, s):
                sp.dma_start(xt[:, s, :], rows(x_f, h)).then_inc(tile_in[s], 16)
                sp.dma_start(ct[:, s, :], rows(c_f, h)).then_inc(tile_in[s], 16)
                win = krev[h, 0:L]
                sp.dma_start(gr[:, s, :], bass.AP(win.tensor, win.offset, [[1, P], [1, L]])).then_inc(tile_in[s], 16)
                row = skip_v[h]
                sp.dma_start(skip_c[:, s, :], bass.AP(row.tensor, row.offset, [[0, B], [1, NH], [1, 1]])).then_inc(tile_in[s], 16)

            def store(h, s):
                sp.wait_ge(x1_ready, h + 1)
                sp.dma_start(rows(x1_rows, h), x1[:, s, :]).then_inc(x1_out[s], 16)
                sp.wait_ge(xn_ready, h + 1)
                sp.dma_start(rows(xn_rows[0:T, :], h), xn[:, s, :]).then_inc(xn_out[s], 16)

            def iteration(h, s, first=False, fetch=True):
                if fetch:
                    sp.wait_ge(xr_ready, h + 1)
                    sp.wait_ge(g_ready, h + 1)
                    load(h + 2, s)
                if not first:
                    store(h - 1, 1 - s)

            load(0, 0)
            load(1, 1)
            iteration(0, 0, first=True)
            sp.wait_ge(w_sb, 1 + 2 * NC + n_up)
            for r in range(NW):
                weights(sp, r, r)
            iteration(1, 1)
            with sp.Fori(0, 14) as i:
                iteration(i * 2 + 2, 0)
                iteration(i * 2 + 3, 1)
            iteration(NT - 2, 0, fetch=False)
            iteration(NT - 1, 1, fetch=False)
            store(NT - 1, 1)

            def b_load_xn(t, s, first=False):
                if not first:
                    sp.wait_ge(b_xT_ps, t - 1)
                sp.wait_ge(xn_out[s], landed(t, s, 16))
                sp.dma_start(xn[:, s, :], rows(xn_rows[0:T, :], t)).then_inc(b_xn_in[s], 16)

            def b_load_x1(t, s):
                sp.wait_ge(x1_out[s], landed(t, s, 16))
                sp.dma_start(xr[:, s, :], rows(x1_rows, t)).then_inc(b_x1_in[s], 16)

            def b_store(t, s):
                sp.wait_ge(y_ready, t + 1)
                sp.dma_start(rows(out[0:T, :], t), y[:, s, :]).then_inc(y_out[s], 16)

            sp.wait_ge(xT_ps, NT)
            for t in range(2):
                b_load_xn(t, t, first=True)
                b_load_x1(t, t)

            def b_iteration(t, s, fetch_xn=True, fetch_x1=True):
                if fetch_xn:
                    b_load_xn(t + 2, s)
                if not among(t, 0):
                    b_store(t - 1, 1 - s)
                    if fetch_x1:
                        b_load_x1(t + 1, 1 - s)

            b_iteration(0, 0)
            b_iteration(1, 1)
            with sp.Fori(1, NT // 2 - 1) as i:
                b_iteration(i * 2, 0)
                b_iteration(i * 2 + 1, 1)
            b_iteration(NT - 2, 0, fetch_xn=False)
            b_iteration(NT - 1, 1, fetch_xn=False, fetch_x1=False)
            b_store(NT - 1, 1)

            for s in range(2):
                sp.wait_ge(placed[s], NT // 2 * K * 16)
            sp.dma_start(tbl[:].rearrange("p e c -> p (e c)"),
                         table.rearrange("(p e) c -> p (e c)", e=E)).then_inc(table_in, 16)

            with sp.Fori(0, E // NW - 1) as i:
                for r in range(NW):
                    sp.wait_ge(c_down, i * NW + r + 1)
                    weights(sp, i * NW + r + NW, r)

        @block.tensor
        def _(pe):
            pe.wait_ge(consts_in, 16)
            pe.wait_ge(gate_w_in, 16)
            for c in range(NC):
                last = pe.transpose(Y[0][:, c * E:(c + 1) * E], gate_in[:, c * P:(c + 1) * P], ident[0:E, 0:E])
            last.then_inc(w_ps, 1)

            def transposes(h, s):
                pe.wait_ge(v_ready, h + 1)
                for c in range(NC):
                    last = pe.transpose(TA[:, c * P:(c + 1) * P], v[:, s, c * P:(c + 1) * P], ident)
                last.then_inc(vT_ps, 1)
                for c in range(NC):
                    last = pe.transpose(TB[:, c * P:(c + 1) * P], ct[:, s, c * P:(c + 1) * P], ident)
                last.then_inc(cT_ps, 1)
                pe.wait_ge(w_ready, h + 1)
                pe.matmul(DX[:, :], same_b, w[:, s, :], start=True, stop=True).then_inc(dx_ps, 1)

            def conv(h, s, c, half, first=False):
                u = 2 * c + half
                if half == 0:
                    pe.wait_ge(kv_ready, h * NC + c + 1)
                    if c == 0:
                        pe.wait_ge(g_ready, h + 1)
                if not (first and u < 4):
                    pe.wait_ge(z_done, h * 8 + u - 3)
                for a in range(c + 1):
                    d = c - a
                    last = pe.matmul(Y[u % 4][:, :], toep[:, s, d * P:(d + 1) * P], kv[:, s, a, half * 512:(half + 1) * 512],
                                     start=(a == 0), stop=(a == c))
                last.then_inc(conv_done, 1)

            def turn_o(h, s):
                pe.wait_ge(o_done, h * 8 + 8)
                for c in range(NC):
                    last = pe.transpose(OT[:, c * P:(c + 1) * P], o[:, s, c, :], ident)
                last.then_inc(oT_ps, 1)

            def turn_xn(h, s):
                pe.wait_ge(xn_ready, h + 1)
                for c in range(NC):
                    last = pe.transpose(TA[:, c * P:(c + 1) * P], xn[:, s, c * P:(c + 1) * P], ident)
                last.then_inc(xT_ps, 1)

            def router(h, s):
                pe.wait_ge(xT_sb, h + 1)
                for c in range(NC):
                    last = pe.matmul(DX[:, 0:E], xT[:, s, c, :], gateT[:, c, :], start=(c == 0), stop=(c == NC - 1))
                last.then_inc(logit_ps, 1)

            def iteration(h, s, first=False, last=False):
                for c in range(2):
                    for half in range(2):
                        conv(h, s, c, half, first)
                if not first:
                    turn_o(h - 1, 1 - s)
                if not last:
                    pe.wait_ge(vT_sb, h + 1)
                    pe.wait_ge(cT_sb, h + 1)
                    if not among(h, 0, 1):
                        pe.wait_ge(xT_sb, h - 1)
                        pe.wait_ge(sc_ready, h - 1)
                    transposes(h + 1, 1 - s)
                for half in range(2):
                    conv(h, s, 2, half, first)
                if not first:
                    if not last:
                        pe.wait_ge(vT_sb, h + 2)
                    turn_xn(h - 1, 1 - s)
                conv(h, s, 3, 0, first)
                if not first:
                    if not last:
                        pe.wait_ge(dc_ready, h + 2)
                    router(h - 1, 1 - s)
                conv(h, s, 3, 1, first)

            transposes(0, 0)
            pe.wait_ge(sh_gu_in, 32)
            for c in range(NC):
                for g in range(2):
                    n = 2 * c + g
                    if n >= 3:
                        pe.wait_ge(w_sb, n - 2)
                    for a in range(n_up):
                        last = pe.transpose(Y[(n + 1) % 4][:, a * P:(a + 1) * P],
                                            ring[:, g, a * L + c * P:a * L + (c + 1) * P], ident)
                    last.then_inc(w_ps, 1)
            pe.wait_ge(sh_down_in, 16)
            for a in range(n_up):
                n = 2 * NC + a
                pe.wait_ge(w_sb, n - 2)
                for c in range(NC):
                    last = pe.transpose(Y[(n + 1) % 4][:, c * P:(c + 1) * P],
                                        ring[:, 2, c * SI + a * P:c * SI + (a + 1) * P], ident)
                last.then_inc(w_ps, 1)
            pe.wait_ge(w_sb, 1 + 2 * NC + n_up)
            iteration(0, 0, first=True)
            iteration(1, 1)
            with pe.Fori(0, 14) as i:
                iteration(i * 2 + 2, 0)
                iteration(i * 2 + 3, 1)
            iteration(NT - 2, 0)
            iteration(NT - 1, 1, last=True)
            turn_o(NT - 1, 1)
            turn_xn(NT - 1, 1)
            pe.wait_ge(sc_ready, NT - 1)
            router(NT - 1, 1)

            pe.wait_ge(z_done, 8 * NT)
            pe.wait_ge(pre_ready, NT)
            pe.wait_ge(dve_setup, 6)
            for g in range(4):
                t8 = slice(8 * g, 8 * g + 8)
                pe.matmul(Y[g][:, :], sq16[:, 0, :], pre[:, t8, :], start=True, stop=False)
                pe.matmul(Y[g][:, :], sq16[:, 1, :], mask[:, t8, :], start=False, stop=False)
                pe.matmul(Y[g][:, :], sq16[:, 2, :], pre[:, NT:NT + 1, :].to_broadcast([P, 8, E]),
                          start=False, stop=True).then_inc(pos_ps, 1)

            def b_turn(t, s):
                pe.wait_ge(b_xn_in[s], landed(t, s, 16))
                for c in range(NC):
                    last = pe.transpose(TA[:, c * P:(c + 1) * P], xn[:, s, c * P:(c + 1) * P], ident)
                last.then_inc(b_xT_ps, 1)

            def b_half(t, s, g):
                for c in range(NC):
                    last = pe.matmul(Y[2 * s + g][:, 0:SI], xT[:, s, c, :], sh_guT[:, c, g * SI:(g + 1) * SI],
                                     start=(c == 0), stop=(c == NC - 1))
                last.then_inc(up_ps if g else gate_ps, 1)

            def b_turn_hid(t, s):
                pe.wait_ge(b_hid, t + 1)
                for a in range(n_up):
                    last = pe.transpose(TB[:, a * P:(a + 1) * P], hid[:, s, a * P:(a + 1) * P], ident)
                last.then_inc(b_hT_ps, 1)

            def b_out(t, s):
                pe.wait_ge(b_hT_sb, t + 1)
                for a in range(n_up):
                    last = pe.matmul(DN[s][:, :], hT[:, s, a, :], sh_dT[:, a, :], start=(a == 0), stop=(a == n_up - 1))
                last.then_inc(b_down, 1)

            def b_iteration(t, s, first=False, last=False):
                pe.wait_ge(b_xT_sb, t + 1)
                if not last:
                    b_turn(t + 1, 1 - s)
                if first:
                    pe.wait_ge(pos_sb, 4)
                elif not among(t, 1):
                    pe.wait_ge(b_hid, t - 1)
                b_half(t, s, 0)
                if not first:
                    b_turn_hid(t - 1, 1 - s)
                b_half(t, s, 1)
                if not first:
                    if among(t, 1):
                        pe.wait_ge(x1_ready, NT)
                        pe.wait_ge(sc_ready, NT)
                    elif not among(t, 2):
                        pe.wait_ge(y_ready, t - 2)
                    b_out(t - 1, 1 - s)

            b_turn(0, 0)
            b_iteration(0, 0, first=True)
            b_iteration(1, 1)
            b_iteration(2, 0)
            with pe.Fori(0, 14) as i:
                b_iteration(i * 2 + 3, 1)
                b_iteration(i * 2 + 4, 0)
            b_iteration(NT - 1, 1, last=True)
            b_turn_hid(NT - 1, 1)
            pe.wait_ge(y_ready, NT - 2)
            b_out(NT - 1, 1)

            def c_turn(e, s):
                pe.wait_ge(gathered[s], landed(e, s, 16))
                for c in range(NC):
                    last = pe.transpose(TA[:, c * P:(c + 1) * P], xg[:, s, c * P:(c + 1) * P], ident)
                last.then_inc(c_xT_ps, 1)

            def c_up(e, s, r, part):
                for c in range(2 * part, 2 * part + 2):
                    last = pe.matmul(Y[s][:, 0:SI], xT[:, s, c, :], ring[:, r, c * SI:(c + 1) * SI],
                                     start=(c == 0), stop=(c == NC - 1))
                if part:
                    last.then_inc(c_gu, 1)

            def c_turn_hid(e, s):
                pe.wait_ge(c_hid, e + 1)
                for a in range(2):
                    last = pe.transpose(TB[0:IH, a * P:(a + 1) * P], hid[:, s, a * IH:(a + 1) * IH], ident)
                last.then_inc(c_hT_ps, 1)

            def c_out(e, s, r):
                pe.wait_ge(c_hT_sb, e + 1)
                for a in range(2):
                    o_w = NC * SI + a * L
                    last = pe.matmul(DN[s][:, :], hT[0:IH, s, a, :], ring[0:IH, r, o_w:o_w + L], start=(a == 0), stop=(a == 1))
                last.then_inc(c_down, 1)

            def c_iteration(e, s, r, first=False, last=False):
                pe.wait_ge(c_xT_sb, e + 1)
                if not last:
                    c_turn(e + 1, 1 - s)
                pe.wait_ge(weights_in[r], (e - r) * 8 + 32)
                if not (first or among(e, 1)):
                    pe.wait_ge(c_hid, e - 1)
                c_up(e, s, r, 0)
                if not first:
                    c_turn_hid(e - 1, 1 - s)
                c_up(e, s, r, 1)
                if not first:
                    if not among(e, 1, 2):
                        pe.wait_ge(eo_ready, e - 2)
                    c_out(e - 1, 1 - s, (r + NW - 1) % NW)

            pe.wait_ge(b_xT_sb, NT)
            c_turn(0, 0)
            pe.wait_ge(y_ready, NT)
            for e in range(4):
                c_iteration(e, e % 2, e % NW, first=(e == 0))
            with pe.Fori(1, E // NW - 1) as i:
                for r in range(NW):
                    c_iteration(i * NW + r, r % 2, r)
            for e in range(E - NW, E):
                c_iteration(e, e % 2, e % NW, last=(e == E - 1))
            c_turn_hid(E - 1, 1)
            pe.wait_ge(eo_ready, E - 2)
            c_out(E - 1, 1, NW - 1)

        @block.scalar
        def _(act):
            act.wait_ge(small_in, 48)
            act.wait_ge(dve_setup, 3)
            act.activation(kpad[:, 0:L], z[0:NT, 0, ::-1], ACT.Copy).then_inc(krev_ready, 1)

            def sqrt1(h):
                act.wait_ge(ln1_mv, h + 1)
                act.activation(sd1[:], mv1[:, 1:2], ACT.Sqrt, bias=eps[:, 0:1]).then_inc(ln1_sd, 1)

            def filter_blocks(h, s, first=False):
                act.wait_ge(tile_in[s], landed(h, s, 64))
                if not first:
                    act.wait_ge(conv_done, h * 8 - 8)
                act.activation(toep[:, s, :], gr[:, s, ::-1], ACT.Copy).then_inc(g_ready, 1)

            def evacuate(h, s, first=False):
                act.wait_ge(vT_ps, h + 1)
                if not first:
                    act.wait_ge(kv_ready, h * NC - NC)
                act.activation(vT[:, s, :, :].rearrange("p c n -> p (c n)"), TA[:, :], ACT.Copy).then_inc(vT_sb, 1)
                act.wait_ge(cT_ps, h + 1)
                if not first:
                    act.wait_ge(z_done, h * 8 - 8)
                act.activation(cT[:, s, :, :].rearrange("p c n -> p (c n)"), TB[:, :], ACT.Copy).then_inc(cT_sb, 1)

            def sqrt2(h):
                act.wait_ge(ln2_mv, h + 1)
                act.activation(sd2[:], mv2[:, 1:2], ACT.Sqrt, bias=eps[:, 0:1]).then_inc(ln2_sd, 1)

            def evacuate_xn(h, s, first=False):
                act.wait_ge(xT_ps, h + 1)
                if not first:
                    act.wait_ge(logit_ps, h - 1)
                act.activation(xT[:, s, :, :].rearrange("p c n -> p (c n)"), TA[:, :], ACT.Copy).then_inc(xT_sb, 1)

            def keep_scores(h):
                act.wait_ge(sc_ready, h + 1)
                act.activation(sc_all[:, bass.ds(h, 1), :].rearrange("p a e -> p (a e)"), sc[:], ACT.Copy).then_inc(sc_kept, 1)
                act.wait_ge(s8_ready, h + 1)
                act.activation(s8_all[:, bass.ds(h, 1), :].rearrange("p a e -> p (a e)"), s8[:], ACT.Copy).then_inc(sc_kept, 1)

            sqrt1(0)
            act.wait_ge(w_ps, 1)
            act.activation(gateT[:].rearrange("p c e -> p (c e)"), Y[0][:, 0:NC * E], ACT.Copy).then_inc(w_sb, 1)
            filter_blocks(0, 0, first=True)
            evacuate(0, 0, first=True)
            for c in range(NC):
                for g in range(2):
                    n = 1 + 2 * c + g
                    act.wait_ge(w_ps, n + 1)
                    act.activation(sh_guT[:, c, g * SI:(g + 1) * SI], Y[n % 4][:, 0:SI], ACT.Copy).then_inc(w_sb, 1)
            for a in range(n_up):
                n = 1 + 2 * NC + a
                act.wait_ge(w_ps, n + 1)
                act.activation(sh_dT[:, a, :], Y[n % 4][:, :], ACT.Copy).then_inc(w_sb, 1)

            def iteration(h, s, first=False, last=False):
                if not first:
                    if not among(h, 1):
                        keep_scores(h - 2)
                if not last:
                    sqrt1(h + 1)
                    filter_blocks(h + 1, 1 - s, first=first)
                    evacuate(h + 1, 1 - s, first=first)
                if not first:
                    sqrt2(h - 1)
                    evacuate_xn(h - 1, 1 - s, first=among(h, 1, 2))

            iteration(0, 0, first=True)
            iteration(1, 1)
            iteration(2, 0)
            with act.Fori(0, 14) as i:
                iteration(i * 2 + 3, 1)
                iteration(i * 2 + 4, 0)
            iteration(NT - 1, 1, last=True)
            keep_scores(NT - 2)
            sqrt2(NT - 1)
            evacuate_xn(NT - 1, 1)
            keep_scores(NT - 1)

            act.wait_ge(sc_kept, 2 * NT)
            act.activation(sc_all[:].rearrange("p t e -> p (t e)"), sc_all[:].rearrange("p t e -> p (t e)"), ACT.Exp).then_inc(exp_ready, 1)
            act.activation(s8_all[:].rearrange("p t e -> p (t e)"), s8_all[:].rearrange("p t e -> p (t e)"), ACT.Exp).then_inc(exp_ready, 1)
            for g in range(4):
                act.wait_ge(pos_ps, g + 1)
                act.activation(pos[:, 8 * g:8 * g + 8, :].rearrange("p t e -> p (t e)"), Y[g][:, :], ACT.Copy).then_inc(pos_sb, 1)

            def b_evacuate(t, s, first=False):
                act.wait_ge(b_xT_ps, t + 1)
                if first:
                    act.wait_ge(logit_ps, NT)
                else:
                    act.wait_ge(up_ps, t - 1)
                act.activation(xT[:, s, :, :].rearrange("p c n -> p (c n)"), TA[:, :], ACT.Copy).then_inc(b_xT_sb, 1)

            def b_gate(t, s):
                act.wait_ge(gate_ps, t + 1)
                if not among(t, 0, 1):
                    act.wait_ge(b_hid, t - 1)
                act.activation(sg[:, s, :], Y[2 * s][:, 0:SI], ACT.Silu).then_inc(b_silu, 1)

            def b_evacuate_hid(t, s):
                act.wait_ge(b_hT_ps, t + 1)
                if not among(t, 0, 1):
                    act.wait_ge(b_down, t - 1)
                act.activation(hT[:, s, :, :].rearrange("p c n -> p (c n)"), TB[:, 0:SI], ACT.Copy).then_inc(b_hT_sb, 1)

            def b_iteration(t, s, first=False, last=False):
                if not last:
                    b_evacuate(t + 1, 1 - s, first=first)
                b_gate(t, s)
                if not first:
                    b_evacuate_hid(t - 1, 1 - s)

            act.wait_ge(conv_done, 8 * NT)
            b_evacuate(0, 0, first=True)
            b_iteration(0, 0, first=True)
            b_iteration(1, 1)
            b_iteration(2, 0)
            with act.Fori(0, 14) as i:
                b_iteration(i * 2 + 3, 1)
                b_iteration(i * 2 + 4, 0)
            b_iteration(NT - 1, 1, last=True)
            b_evacuate_hid(NT - 1, 1)

            def c_evacuate(e, s, first=False):
                act.wait_ge(c_xT_ps, e + 1)
                if first:
                    act.wait_ge(up_ps, NT)
                else:
                    act.wait_ge(c_gu, e - 1)
                act.activation(xT[:, s, :, :].rearrange("p c n -> p (c n)"), TA[:, :], ACT.Copy).then_inc(c_xT_sb, 1)

            def c_gate(e, s):
                act.wait_ge(c_gu, e + 1)
                if among(e, 0):
                    act.wait_ge(b_hid, NT)
                elif not among(e, 1):
                    act.wait_ge(c_hid, e - 1)
                act.activation(sg[:, s, 0:I], Y[s][:, 0:I], ACT.Silu).then_inc(c_silu, 1)

            def c_evacuate_hid(e, s):
                act.wait_ge(c_hT_ps, e + 1)
                if among(e, 0):
                    act.wait_ge(b_down, NT)
                elif not among(e, 1):
                    act.wait_ge(c_down, e - 1)
                act.activation(hT[0:IH, s, 0:2, :].rearrange("p c n -> p (c n)"), TB[0:IH, 0:2 * P], ACT.Copy).then_inc(c_hT_sb, 1)

            def c_iteration(e, s, last=False):
                if not last:
                    c_evacuate(e + 1, 1 - s, first=(among(e, 0)))
                if not among(e, 0):
                    c_evacuate_hid(e - 1, 1 - s)
                c_gate(e, s)

            c_evacuate(0, 0, first=True)
            for e in range(3):
                c_iteration(e, e % 2)
            with act.Fori(0, (E - 4) // 2) as i:
                c_iteration(i * 2 + 3, 1)
                c_iteration(i * 2 + 4, 0)
            c_iteration(E - 1, 1, last=True)
            c_evacuate_hid(E - 1, 1)

        @block.gpsimd
        def _(pool):
            def form_kv(h, s, first=False):
                pool.wait_ge(vT_sb, h + 1)
                pool.wait_ge(cT_sb, h + 1)
                if not first:
                    pool.wait_ge(conv_done, h * 8 - 8)
                for c in range(NC):
                    a = vT[:, s, c, :].rearrange("p (b i) -> p b i", i=NH).unsqueeze(3).to_broadcast([P, B, NH, NH])
                    d = cT[:, s, c, :].rearrange("p (b j) -> p b j", j=NH).unsqueeze(2).to_broadcast([P, B, NH, NH])
                    pool.tensor_tensor(kv[:, s, c, :].rearrange("p (b i j) -> p b i j", i=NH, j=NH), a, d,
                                       ALU.mult).then_inc(kv_ready, 1)

            form_kv(0, 0, first=True)
            form_kv(1, 1, first=True)
            with pool.Fori(1, NT // 2) as i:
                form_kv(i * 2, 0)
                form_kv(i * 2 + 1, 1)

            pool.wait_ge(pads_out, 48)

            def place(t, s):
                pool.wait_ge(slot_ready, t * 2 + 2)
                pool.sem_inc(pool_turn, 1)
                for c in range(K):
                    pool.indirect_dma_start(
                        out=table, out_offset=bass.IndirectOffsetOnAxis(ap=slot[:, s, c:c + 1], axis=0),
                        in_=recs[:, s, c, :], in_offset=None, bounds_check=CAP * E - 1, oob_is_err=False,
                    ).then_inc(placed[s], 16)

            with pool.Fori(0, NT // 2) as i:
                place(i * 2, 0)
                place(i * 2 + 1, 1)

            def fetch(e, s, r):
                pool.tensor_copy(idx4[:, r:r + 1], idx_i[:, bass.ds(e, 1)]).then_inc(idx4_ready, 1)
                pool.wait_ge(idx4_ready, e + 1)
                if not among(e, 0, 1):
                    pool.wait_ge(c_xT_ps, e - 1)
                pool.sem_inc(pool_turn, 1)
                pool.indirect_dma_start(out=xg[:, s, :], out_offset=None, in_=xn_rows,
                                        in_offset=bass.IndirectOffsetOnAxis(ap=idx4[:, r:r + 1], axis=0),
                                        ).then_inc(gathered[s], 16)

            def add(e, s, r):
                pool.wait_ge(eo_ready, e + 1)
                if not among(e, 0):
                    pool.wait_ge(added, e * 16)
                pool.sem_inc(pool_turn, 1)
                pool.indirect_dma_start(out=out, out_offset=bass.IndirectOffsetOnAxis(ap=idx4[:, r:r + 1], axis=0),
                                        in_=y[:, s, :], in_offset=None, compute_op=ALU.add).then_inc(added, 16)

            pool.wait_ge(idx_i_ready, 1)
            pool.wait_ge(conv_done, 8 * NT)
            for s in range(2):
                pool.wait_ge(xn_out[s], NT // 2 * 16)
            fetch(0, 0, 0)
            fetch(1, 1, 1)
            for s in range(2):
                pool.wait_ge(y_out[s], NT // 2 * 16)
            fetch(2, 0, 2)
            add(0, 0, 0)
            fetch(3, 1, 3)
            add(1, 1, 1)
            with pool.Fori(0, (E - 4) // 4) as i:
                for n in range(4):
                    fetch(i * 4 + n + 4, n % 2, n)
                    add(i * 4 + n + 2, n % 2, (n + 2) % 4)
            for e in range(E - 2, E):
                add(e, e % 2, e % 4)
            pool.wait_ge(added, E * 16)

        @block.vector
        def _(dve):
            dve.memset(zeros[:], 0.0).then_inc(dve_setup, 1)
            dve.memset(kpad[:], 0.0).then_inc(dve_setup, 1)
            dve.memset(eps[:], EPS).then_inc(dve_setup, 1)
            dve.memset(pre[:, 0, :], 0.0).then_inc(dve_setup, 1)
            dve.wait_ge(consts_in, 16)
            dve.tensor_copy(sq16[:].rearrange("p a n -> p (a n)"), sq[:, 1:4, :].rearrange("p a n -> p (a n)")).then_inc(dve_setup, 2)

            def layernorm(src, st, mv, sd, rs, dst, n, stats, mean, root, rstd, ready):
                dve.bn_stats(st[:], src).then_inc(stats, 1)
                dve.wait_ge(stats, n + 1)
                dve.sem_inc(dve_turn, 1)
                dve.bn_aggr(mv[:], st[:]).then_inc(mean, 1)
                dve.wait_ge(root, n + 1)
                dve.reciprocal(rs[:], sd[:]).then_inc(rstd, 1)
                dve.wait_ge(rstd, n + 1)
                dve.tensor_scalar(dst, src, mv[:, 0:1], rs[:, 0:1], ALU.subtract, ALU.mult).then_inc(ready, 1)

            def ln1(h, s):
                dve.wait_ge(tile_in[s], landed(h, s, 64))
                layernorm(xt[:, s, :], st1, mv1, sd1, rs1, v[:, s, :], h, ln1_stats, ln1_mv, ln1_sd, ln1_rstd, v_ready)
                dve.wait_ge(v_ready, h + 1)
                dve.scalar_tensor_tensor(w[:, s, :], v[:, s, :], skip_c[:, s, :], ct[:, s, :], ALU.mult, ALU.mult).then_inc(w_ready, 1)

            def sum_i(h, s, c):
                for half in range(2):
                    u = 2 * c + half
                    dve.wait_ge(conv_done, h * 8 + u + 1)
                    m = cT[:, s, c, half * 64:(half + 1) * 64].unsqueeze(2).to_broadcast([P, 64, NH])
                    if not (among(h, 0) and u < 4):
                        dve.wait_ge(o_done, h * 8 + u - 3)
                    dve.tensor_tensor(z[:, u % 4, :].rearrange("p (n j) -> p n j", j=NH),
                                      Y[u % 4][:, :].rearrange("p (n j) -> p n j", j=NH), m, ALU.mult).then_inc(z_done, 1)
                for half in range(2):
                    u = 2 * c + half
                    dve.wait_ge(z_done, h * 8 + u + 1)
                    dve.tensor_reduce(o[:, s, c, half * 64:(half + 1) * 64].rearrange("p (b j) -> p b j", j=NH),
                                      z[:, u % 4, :].rearrange("p (b i j) -> p b j i", i=NH, j=NH), AX.X, ALU.add).then_inc(o_done, 1)

            def residual(h, s):
                dve.wait_ge(dx_ps, h + 1)
                dve.tensor_tensor(w[:, s, :], DX[:, :], ct[:, s, :], ALU.mult).then_inc(dc_ready, 1)
                dve.wait_ge(dc_ready, h + 1)
                dve.tensor_tensor(xr[:, s, :], w[:, s, :], xt[:, s, :], ALU.add).then_inc(xr_ready, 1)

            def finish_x1(h, s, first=False):
                dve.wait_ge(oT_ps, h + 1)
                dve.wait_ge(xr_ready, h + 1)
                if not first:
                    dve.wait_ge(x1_out[s], landed(h - 2, s, 16))
                    dve.wait_ge(xn_out[s], landed(h - 2, s, 16))
                dve.tensor_tensor(x1[:, s, :], OT[:, :], xr[:, s, :], ALU.add).then_inc(x1_ready, 1)
                dve.wait_ge(x1_ready, h + 1)
                layernorm(x1[:, s, :], st2, mv2, sd2, rs2, xn[:, s, :], h, ln2_stats, ln2_mv, ln2_sd, ln2_rstd, xn_ready)

            def choose(h, first=False):
                dve.wait_ge(logit_ps, h + 1)
                dve.sem_inc(dve_turn, 1)
                dve.max(m8[:], DX[:, 0:E]).then_inc(max_ready, 1)
                dve.wait_ge(max_ready, h + 1)
                if not first:
                    dve.wait_ge(sc_kept, h * 2)
                dve.tensor_scalar(sc[:], DX[:, 0:E], m8[:, 0:1], FLOOR, ALU.subtract, ALU.max).then_inc(sc_ready, 1)
                dve.wait_ge(sc_ready, h + 1)
                dve.sem_inc(dve_turn, 1)
                dve.max(s8[:], sc[:]).then_inc(s8_ready, 1)
                dve.wait_ge(s8_ready, h + 1)
                dve.sem_inc(dve_turn, 1)
                dve.max_index(i8[:], s8[:], sc[:]).then_inc(i8_ready, 1)
                dve.wait_ge(i8_ready, h + 1)
                idx = idx_all[:, bass.ds(h, 1), :].rearrange("p a k -> p (a k)")
                dve.tensor_copy(idx, i8[:, 0:K]).then_inc(idx_ready, 1)
                dve.wait_ge(idx_ready, h + 1)
                oh = onehot[:, bass.ds(h, 1), :, :].rearrange("p a k e -> p (a k) e")
                dve.tensor_tensor(oh, iota[:].unsqueeze(1).to_broadcast([P, K, E]), idx.unsqueeze(2).to_broadcast([P, K, E]),
                                  ALU.is_equal).then_inc(onehot_ready, 1)
                dve.wait_ge(onehot_ready, h + 1)
                mk = mask[:, bass.ds(h, 1), :].rearrange("p a e -> p (a e)")
                dve.tensor_reduce(mk, oh.rearrange("p k e -> p e k"), AX.X, ALU.max).then_inc(mask_ready, 1)
                dve.wait_ge(mask_ready, h + 1)
                dve.tensor_tensor(pre[:, bass.ds(h + 1, 1), :], pre[:, bass.ds(h, 1), :], mask[:, bass.ds(h, 1), :],
                                  ALU.add).then_inc(pre_ready, 1)

            def iteration(h, s, first=False, last=False):
                if not last:
                    ln1(h + 1, 1 - s)
                sum_i(h, s, 0)
                sum_i(h, s, 1)
                if not first:
                    finish_x1(h - 1, 1 - s, first=among(h, 1, 2))
                if not last:
                    residual(h + 1, 1 - s)
                sum_i(h, s, 2)
                sum_i(h, s, 3)
                if not first:
                    choose(h - 1, first=(among(h, 1)))

            dve.wait_ge(small_in, 48)
            ln1(0, 0)
            residual(0, 0)
            iteration(0, 0, first=True)
            iteration(1, 1)
            iteration(2, 0)
            with dve.Fori(0, 14) as i:
                iteration(i * 2 + 3, 1)
                iteration(i * 2 + 4, 0)
            iteration(NT - 1, 1, last=True)
            finish_x1(NT - 1, 1)
            choose(NT - 1)

            dve.wait_ge(exp_ready, 2)
            dve.tensor_reduce(sums[:], sc_all[:], AX.X, ALU.add).then_inc(sums_ready, 1)
            dve.wait_ge(sums_ready, 1)
            dve.reciprocal(rinv[:], sums[:]).then_inc(rinv_ready, 1)
            dve.wait_ge(rinv_ready, 1)
            dve.tensor_tensor(rec[:, :, :, 1], s8_all[:, :, 0:K], rinv[:].unsqueeze(2).to_broadcast([P, NT, K]),
                              ALU.mult).then_inc(rec_ready, 1)
            dve.wait_ge(rec_ready, 1)
            dve.wait_ge(pos_sb, 4)

            def place(t, s, first=False):
                dve.tensor_tensor(prod[:], onehot[:, bass.ds(t, 1), :, :].rearrange("p a k e -> p (a k) e"),
                                  pos[:, bass.ds(t, 1), :].to_broadcast([P, K, E]), ALU.mult).then_inc(prod_ready, 1)
                dve.wait_ge(prod_ready, t + 1)
                dve.tensor_reduce(pk[:], prod[:], AX.X, ALU.add).then_inc(pk_ready, 1)
                dve.wait_ge(pk_ready, t + 1)
                if not first:
                    dve.wait_ge(placed[s], landed(t - 2, s, K * 16))
                dve.scalar_tensor_tensor(slot[:, s, :], pk[:], float(E), idx_all[:, bass.ds(t, 1), :].rearrange("p a k -> p (a k)"),
                                         ALU.mult, ALU.add).then_inc(slot_ready, 1)
                dve.tensor_copy(recs[:, s, :, :].rearrange("p k c -> p (k c)"),
                                rec[:, bass.ds(t, 1), :, :].rearrange("p a k c -> p (a k c)")).then_inc(slot_ready, 1)

            def b_hidden(t, s):
                dve.wait_ge(b_silu, t + 1)
                dve.wait_ge(up_ps, t + 1)
                if not among(t, 0, 1):
                    dve.wait_ge(b_hT_ps, t - 1)
                dve.tensor_tensor(hid[:, s, :], Y[2 * s + 1][:, 0:SI], sg[:, s, :], ALU.mult).then_inc(b_hid, 1)

            def b_result(t, s):
                dve.wait_ge(b_down, t + 1)
                dve.wait_ge(b_x1_in[s], landed(t, s, 16))
                if not among(t, 0, 1):
                    dve.wait_ge(y_out[s], landed(t - 2, s, 16))
                dve.tensor_tensor(y[:, s, :], DN[s][:, :], xr[:, s, :], ALU.add).then_inc(y_ready, 1)

            def b_iteration(t, s, first=False):
                place(t, s, first=among(t, 0, 1))
                b_hidden(t, s)
                if not first:
                    b_result(t - 1, 1 - s)

            b_iteration(0, 0, first=True)
            b_iteration(1, 1)
            b_iteration(2, 0)
            with dve.Fori(0, 14) as i:
                b_iteration(i * 2 + 3, 1)
                b_iteration(i * 2 + 4, 0)
            b_iteration(NT - 1, 1)
            b_result(NT - 1, 1)

            dve.wait_ge(table_in, 16)
            dve.tensor_copy(idx_i[:], tbl[:, :, 0]).then_inc(idx_i_ready, 1)

            def c_hidden(e, s):
                dve.wait_ge(c_silu, e + 1)
                if among(e, 0):
                    dve.wait_ge(b_hT_ps, NT)
                elif not among(e, 1):
                    dve.wait_ge(c_hT_ps, e - 1)
                dve.tensor_tensor(hid[:, s, 0:I], Y[s][:, I:2 * I], sg[:, s, 0:I], ALU.mult).then_inc(c_hid, 1)

            def c_result(e, s):
                dve.wait_ge(c_down, e + 1)
                if among(e, 0, 1):
                    dve.wait_ge(y_out[s], NT // 2 * 16)
                else:
                    dve.wait_ge(added, e * 16 - 16)
                dve.tensor_scalar(y[:, s, :], DN[s][:, :], tbl[:, bass.ds(e, 1), 1], None, ALU.mult).then_inc(eo_ready, 1)

            def c_iteration(e, s):
                c_hidden(e, s)
                if not among(e, 0):
                    c_result(e - 1, 1 - s)

            for e in range(4):
                c_iteration(e, e % 2)
            with dve.Fori(2, E // 2) as i:
                c_iteration(i * 2, 0)
                c_iteration(i * 2 + 1, 1)
            c_result(E - 1, 1)


_INS = ['x', 'fside_S2_0', 'ctx_2048', 'L0_xattn_k', 'L0_ffn_gate_w', 'L0_ffn_gate_up_proj', 'L0_ffn_down_proj',
        'L0_ffn_shared_gate_w', 'L0_ffn_shared_up_w', 'L0_ffn_shared_down_w']


def constants():
    p = np.arange(P)
    b, j = p // NH, p % NH
    sq = np.stack([np.eye(P), b[:, None] == b[None], (b[:, None] == b[None]) & (j[:, None] < j[None]),
                   b[:, None] < b[None]], 1).astype(np.float32)
    iota = np.tile(np.arange(E, dtype=np.float32), (P, 1))
    rec = np.zeros((P, NT, K, 2), np.float32)
    rec[..., 0] = (b * D + j)[:, None, None] + NH * np.arange(NT)[None, :, None]
    table = np.zeros((CAP, E, 2), np.float32)
    table[..., 0] = T + np.arange(CAP)[:, None]
    return {"sq": sq, "iota": iota, "rec": rec.reshape(P, -1), "table": table.reshape(CAP * E, 2)}


def kernel(**inputs):
    import numpy as _np
    import concourse.bacc as _bacc
    from concourse import mybir as _mybir
    from concourse.bass_utils import run_bass_kernel_spmd as _run

    nc = _bacc.Bacc("TRN2", target_bir_lowering=False, num_devices=1)
    arrays, args = {}, []
    data = [(name, inputs[name]) for name in _INS] + list(constants().items())
    for name, value in data:
        a = _np.ascontiguousarray(value)
        arrays[f"in_{name}_dram"] = a
        args.append(nc.dram_tensor(f"in_{name}_dram", a.shape, _mybir.dt.from_np(a.dtype), kind="ExternalInput").ap())
    args.append(nc.dram_tensor("out_0_dram", (T + CAP, L), _mybir.dt.float32, kind="ExternalOutput").ap())
    build(nc, *args)
    r = _run(nc, [arrays], core_ids=[0])
    return r.results[0]["out_0_dram"][:T].reshape(B, D, L)
```

```python
from contextlib import ExitStack

import numpy as np

import concourse.bass as bass
from concourse import mybir

F32 = mybir.dt.float32
F32R = mybir.dt.float32r
BF16 = mybir.dt.bfloat16
I32 = mybir.dt.int32
U32 = mybir.dt.uint32
ALU = mybir.AluOpType
ACT = mybir.ActivationFunctionType
AX = mybir.AxisListType

P = 128
B, D, L = 16, 256, 512
NH = 8
NT = D // NH
T = B * D
NC = L // P
E, K, CAP = 64, 6, 128
I = 192
SI = 2 * I
IH = I // 2
KVC = B * NH * NH
EPS = 1e-5
FLOOR = -87.3
NW = 4


def build(nc, x, skip, ctx_in, k, gate_w, gate_up, down, sh_gate, sh_up, sh_down,
          c_sq, c_iota, c_rec, c_table, out):
    xn_rows = nc.dram_tensor("xn_rows", [T + CAP, L], F32, kind="Internal").ap()
    x1_rows = nc.dram_tensor("x1_rows", [T, L], F32, kind="Internal").ap()
    krev = nc.dram_tensor("krev", [NT, L + P], F32, kind="Internal").ap()
    table = nc.dram_tensor("table", [CAP * E, 2], F32, kind="Internal").ap()

    with ExitStack() as stack:
        def sb(name, shape, dt=F32):
            return stack.enter_context(nc.sbuf_tensor(name, shape, dt))

        def ps(name):
            return stack.enter_context(nc.psum_tensor(name, [P, 512], F32))

        def sem(name):
            return stack.enter_context(nc.semaphore(name))

        sq = sb("sq", [P, 5, P])
        ident, same_b = sq[:, 0, :], sq[:, 1, :]
        sq16 = sb("sq16", [P, 3, P], BF16)
        iota = sb("iota", [P, E])
        eps = sb("eps", [P, 1])
        zeros = sb("zeros", [P, L])
        kpad = sb("kpad", [NT, L + P])
        gate_in = sb("gate_in", [E, L])
        gateT = sb("gateT", [P, NC, E])
        ring = sb("ring", [P, NW, NC * SI + 2 * L])
        xt = sb("xt", [P, 2, L])
        ct = sb("ct", [P, 2, L])
        gr = sb("gr", [P, 2, L])
        toep = sb("toep", [P, 2, 2, L], F32R)
        skip_c = sb("skip_c", [P, 2, 1])
        v = sb("v", [P, 2, L])
        w = sb("w", [P, 2, L])
        skip_b = sb("skip_b", [P, 2, P])
        vT = sb("vT", [P, 2, NC, P])
        cT = sb("cT", [P, 2, NC, P])
        split = sb("split", [P, 2 * 2 * NC * KVC], F32R)
        kv = split[:].rearrange("p (s a c n) -> p s a c n", s=2, a=2, c=NC)
        kvp = ring[:, 3, 0:2 * KVC].rearrange("p (s n) -> p s n", s=2)
        z = sb("z", [P, 4, 512])
        kin = z[0:NT, 0, :]
        o = sb("o", [P, 2, NC, P])
        xr = sb("xr", [P, 2, L])
        x1 = sb("x1", [P, 2, L])
        xn = sb("xn", [P, 2, L])
        xT = sb("xT", [P, 2, NC, P])
        st1, mv1, sd1, rs1, nb1 = sb("st1", [P, 6]), sb("mv1", [P, 2]), sb("sd1", [P, 1]), sb("rs1", [P, 1]), sb("nb1", [P, 1])
        st2, mv2, sd2, rs2, nb2 = sb("st2", [P, 6]), sb("mv2", [P, 2]), sb("sd2", [P, 1]), sb("rs2", [P, 1]), sb("nb2", [P, 1])
        m8 = sb("m8", [P, 8])
        sc = sb("sc", [P, E])
        s8 = sb("s8", [P, 8])
        i8 = sb("i8", [P, 8], U32)
        sc_all = sb("sc_all", [P, NT, E])
        s8_all = sb("s8_all", [P, NT, 8])
        idx_all = sb("idx_all", [P, NT, K])
        chosen = sb("chosen", [P, K, E], BF16)
        mask = sb("mask", [P, NT, E], BF16)
        pre = sb("pre", [P, NT + 1, E], BF16)
        sums, rinv = sb("sums", [P, NT]), sb("rinv", [P, NT])
        rec = sb("rec", [P, NT, K, 2])
        pk = sb("pk", [P, K])
        slot = sb("slot", [P, 2, K], I32)
        recs = sb("recs", [P, 2, K, 2])
        tbl = sb("tbl", [P, E, 2])
        idx_i = sb("idx_i", [P, E], I32)
        idx_g, idx_a = sb("idx_g", [P, 4], I32), sb("idx_a", [P, 4], I32)
        n_gu, n_d = NC * 2 * SI, SI // P * L
        sh_gu = split[:, 0:2 * n_gu].rearrange("p (a c n) -> p a c n", a=2, c=NC)
        sh_d = split[:, 2 * n_gu:2 * (n_gu + n_d)].rearrange("p (a c n) -> p a c n", a=2, c=SI // P)
        at = 2 * (n_gu + n_d)
        xTs = split[:, at:at + 4 * L].rearrange("p (s a c n) -> p s a c n", s=2, a=2, c=NC)
        hTs = split[:, at + 4 * L:at + 4 * L + 4 * SI].rearrange("p (s a c n) -> p s a c n", s=2, a=2, c=SI // P)
        sg = vT[:].rearrange("p s c n -> p s (c n)")[:, :, 0:SI]
        hid = cT[:].rearrange("p s c n -> p s (c n)")[:, :, 0:SI]
        y = o[:].rearrange("p s c n -> p s (c n)")
        pos = z[:].rearrange("p s (t e) -> p (s t) e", e=E)
        prod = w[:, 0, 0:K * E].rearrange("p (k e) -> p k e", e=E)
        onehot = w[:, 1, 0:K * E].rearrange("p (k e) -> p k e", e=E)
        hT = gr[:, :, 0:2 * P].rearrange("p s (c n) -> p s c n", c=2)
        xg = [xt[:, 0, :], xt[:, 1, :], ct[:, 0, :], ct[:, 1, :]]

        Y = [ps(f"Y{n}") for n in range(4)]
        TA, TB, OT, DX = ps("TA"), ps("TB"), ps("OT"), ps("DX")
        DN = [OT, DX]

        consts_in, small_in = sem("consts_in"), sem("small_in")
        gate_w_in, sh_gu_in, sh_down_in = sem("gate_w_in"), sem("sh_gu_in"), sem("sh_down_in")
        dve_setup, krev_ready, krev_out, pads_out = sem("dve_setup"), sem("krev_ready"), sem("krev_out"), sem("pads_out")
        dve_turn, pool_turn = sem("dve_turn"), sem("pool_turn")
        w_ps, w_sb = sem("w_ps"), sem("w_sb")
        tile_in = [sem("tile_in0"), sem("tile_in1")]
        ln1_stats, ln1_mv, ln1_sd, ln1_rstd = sem("ln1_stats"), sem("ln1_mv"), sem("ln1_sd"), sem("ln1_rstd")
        ln1_nb, ln2_nb, toep_lo, kvp_ready, kv_high = sem("ln1_nb"), sem("ln2_nb"), sem("toep_lo"), sem("kvp_ready"), sem("kv_high")
        skip_ready = sem("skip_ready")
        b_xT_lo, b_hT_lo, sh_lo = sem("b_xT_lo"), sem("b_hT_lo"), sem("sh_lo")
        v_ready, w_ready, g_ready = sem("v_ready"), sem("w_ready"), sem("g_ready")
        vT_ps, cT_ps, dx_ps, vT_sb, cT_sb = sem("vT_ps"), sem("cT_ps"), sem("dx_ps"), sem("vT_sb"), sem("cT_sb")
        kv_ready, conv_done, z_done, o_done = sem("kv_ready"), sem("conv_done"), sem("z_done"), sem("o_done")
        dc_ready, xr_ready, oT_ps, x1_ready = sem("dc_ready"), sem("xr_ready"), sem("oT_ps"), sem("x1_ready")
        ln2_stats, ln2_mv, ln2_sd, ln2_rstd = sem("ln2_stats"), sem("ln2_mv"), sem("ln2_sd"), sem("ln2_rstd")
        xn_ready, xT_ps, xT_sb, logit_ps = sem("xn_ready"), sem("xT_ps"), sem("xT_sb"), sem("logit_ps")
        x1_out, xn_out = [sem("x1_out0"), sem("x1_out1")], [sem("xn_out0"), sem("xn_out1")]
        max_ready, sc_ready, s8_ready, i8_ready = sem("max_ready"), sem("sc_ready"), sem("s8_ready"), sem("i8_ready")
        sc_kept, idx_ready, onehot_ready, b_onehot = sem("sc_kept"), sem("idx_ready"), sem("onehot_ready"), sem("b_onehot")
        mask_ready, pre_ready = sem("mask_ready"), sem("pre_ready")
        pos_ps, pos_sb, exp_ready = sem("pos_ps"), sem("pos_sb"), sem("exp_ready")
        sums_ready, rinv_ready, rec_ready = sem("sums_ready"), sem("rinv_ready"), sem("rec_ready")
        prod_ready, pk_ready, slot_ready = sem("prod_ready"), sem("pk_ready"), sem("slot_ready")
        placed = [sem("placed0"), sem("placed1")]
        b_xn_in, b_x1_in = [sem("b_xn_in0"), sem("b_xn_in1")], [sem("b_x1_in0"), sem("b_x1_in1")]
        b_xT_ps, b_xT_sb, gate_ps, up_ps = sem("b_xT_ps"), sem("b_xT_sb"), sem("gate_ps"), sem("up_ps")
        b_silu, b_hid, b_hT_ps, b_hT_sb, b_down = sem("b_silu"), sem("b_hid"), sem("b_hT_ps"), sem("b_hT_sb"), sem("b_down")
        y_ready, y_out = sem("y_ready"), [sem("y_out0"), sem("y_out1")]
        table_in, idx_i_ready, idx_g_ready, idx_a_ready = sem("table_in"), sem("idx_i_ready"), sem("idx_g_ready"), sem("idx_a_ready")
        weights_in = [sem(f"weights_in{r}") for r in range(NW)]
        gathered = [sem(f"gathered{r}") for r in range(4)]
        c_xT_ps, c_xT_sb, c_gu, c_silu = sem("c_xT_ps"), sem("c_xT_sb"), sem("c_gu"), sem("c_silu")
        c_hid, c_hT_ps, c_hT_sb, c_down = sem("c_hid"), sem("c_hT_ps"), sem("c_hT_sb"), sem("c_down")
        eo_ready, added = sem("eo_ready"), sem("added")

        def rows(dram, h):
            return dram.rearrange("(b h i) l -> h b i l", b=B, i=NH)[h]

        def landed(n, s, each):
            return (n - s) * (each // 2) + each

        def among(n, *numbers):
            return isinstance(n, int) and n in numbers

        x_f = x.rearrange("b d l -> (b d) l")
        c_f = ctx_in.rearrange("b d l -> (b d) l")
        skip_v = skip.rearrange("(h i) -> h i", i=NH)
        n_up = SI // P

        def weights(sp, e, r):
            sp.dma_start(ring[:, r, 0:NC * SI].rearrange("p (c n) -> p c n", c=NC),
                         gate_up[e].rearrange("(c p) n -> p c n", p=P)).then_inc(weights_in[r], 16)
            sp.dma_start(ring[0:IH, r, NC * SI:].rearrange("p (c n) -> p c n", c=2),
                         down[e].rearrange("(c p) n -> p c n", p=IH)).then_inc(weights_in[r], 16)

        block = stack.enter_context(nc.Block())

        @block.sync
        def _(sp):
            sp.dma_start(kin, k).then_inc(small_in, 16)
            sp.dma_start(sq[:, 0:4, :], c_sq).then_inc(consts_in, 16)
            sp.dma_start(gate_in[:], gate_w).then_inc(gate_w_in, 16)
            sp.dma_start(ring[:, 0, 0:n_up * L].rearrange("p (a l) -> p a l", a=n_up),
                         sh_gate.rearrange("(a p) l -> p a l", p=P)).then_inc(sh_gu_in, 16)
            sp.dma_start(ring[:, 1, 0:n_up * L].rearrange("p (a l) -> p a l", a=n_up),
                         sh_up.rearrange("(a p) l -> p a l", p=P)).then_inc(sh_gu_in, 16)
            sp.dma_start(ring[:, 2, 0:NC * SI].rearrange("p (a i) -> p a i", a=NC),
                         sh_down.rearrange("(a p) i -> p a i", p=P)).then_inc(sh_down_in, 16)
            sp.dma_start(iota[:], c_iota).then_inc(small_in, 16)
            sp.dma_start(rec[:].rearrange("p t k c -> p (t k c)"), c_rec).then_inc(small_in, 16)
            sp.wait_ge(dve_setup, 3)
            sp.wait_ge(krev_ready, 1)
            sp.dma_start(krev, kpad[:]).then_inc(krev_out, 16)
            sp.dma_start(table, c_table).then_inc(pads_out, 16)
            sp.dma_start(xn_rows[T:T + CAP, :], zeros[:]).then_inc(pads_out, 16)
            sp.dma_start(out[T:T + CAP, :], zeros[:]).then_inc(pads_out, 16)
            sp.wait_ge(krev_out, 16)

            def load(h, s):
                sp.dma_start(xt[:, s, :], rows(x_f, h)).then_inc(tile_in[s], 16)
                sp.dma_start(ct[:, s, :], rows(c_f, h)).then_inc(tile_in[s], 16)
                win = krev[h, 0:L]
                sp.dma_start(gr[:, s, :], bass.AP(win.tensor, win.offset, [[1, P], [1, L]])).then_inc(tile_in[s], 16)
                row = skip_v[h]
                sp.dma_start(skip_c[:, s, :], bass.AP(row.tensor, row.offset, [[0, B], [1, NH], [1, 1]])).then_inc(tile_in[s], 16)

            def store(h, s):
                sp.wait_ge(x1_ready, h + 1)
                sp.dma_start(rows(x1_rows, h), x1[:, s, :]).then_inc(x1_out[s], 16)
                sp.wait_ge(xn_ready, h + 1)
                sp.dma_start(rows(xn_rows[0:T, :], h), xn[:, s, :]).then_inc(xn_out[s], 16)

            def iteration(h, s):
                if not among(h, NT - 3, NT - 2, NT - 1):
                    sp.wait_ge(xr_ready, h + 2)
                    sp.wait_ge(toep_lo, h + 2)
                    load(h + 3, 1 - s)
                if not among(h, 0):
                    store(h - 1, 1 - s)

            load(0, 0)
            load(1, 1)
            sp.wait_ge(xr_ready, 1)
            sp.wait_ge(toep_lo, 1)
            load(2, 0)
            iteration(0, 0)
            iteration(1, 1)
            iteration(2, 0)
            with sp.Fori(0, 13) as i:
                iteration(i * 2 + 3, 1)
                iteration(i * 2 + 4, 0)
            for h in range(NT - 3, NT):
                iteration(h, h % 2)
            store(NT - 1, 1)

            def b_load_xn(t, s, first=False):
                if not first:
                    sp.wait_ge(b_xT_ps, t - 1)
                sp.wait_ge(xn_out[s], landed(t, s, 16))
                sp.dma_start(xn[:, s, :], rows(xn_rows[0:T, :], t)).then_inc(b_xn_in[s], 16)

            def b_load_x1(t, s):
                sp.wait_ge(x1_out[s], landed(t, s, 16))
                sp.dma_start(xr[:, s, :], rows(x1_rows, t)).then_inc(b_x1_in[s], 16)

            def b_store(t, s):
                sp.wait_ge(y_ready, t + 1)
                sp.dma_start(rows(out[0:T, :], t), y[:, s, :]).then_inc(y_out[s], 16)

            sp.wait_ge(xT_ps, NT)
            for t in range(2):
                b_load_xn(t, t, first=True)
                b_load_x1(t, t)

            sp.wait_ge(sh_lo, 2 * NC + n_up)
            for r in range(NW):
                weights(sp, r, r)

            def b_iteration(t, s, fetch_xn=True, fetch_x1=True):
                if fetch_xn:
                    b_load_xn(t + 2, s)
                if not among(t, 0):
                    b_store(t - 1, 1 - s)
                    if fetch_x1:
                        b_load_x1(t + 1, 1 - s)

            b_iteration(0, 0)
            b_iteration(1, 1)
            with sp.Fori(1, NT // 2 - 1) as i:
                b_iteration(i * 2, 0)
                b_iteration(i * 2 + 1, 1)
            b_iteration(NT - 2, 0, fetch_xn=False)
            b_iteration(NT - 1, 1, fetch_xn=False, fetch_x1=False)
            b_store(NT - 1, 1)

            for s in range(2):
                sp.wait_ge(placed[s], NT // 2 * K * 16)
            sp.dma_start(tbl[:].rearrange("p e c -> p (e c)"),
                         table.rearrange("(p e) c -> p (e c)", e=E)).then_inc(table_in, 16)

            with sp.Fori(0, E // NW - 1) as i:
                for r in range(NW):
                    sp.wait_ge(c_down, i * NW + r + 1)
                    weights(sp, i * NW + r + NW, r)

        @block.tensor
        def _(pe):
            pe.wait_ge(consts_in, 16)
            pe.wait_ge(gate_w_in, 16)
            for c in range(NC):
                last = pe.transpose(Y[0][:, c * E:(c + 1) * E], gate_in[:, c * P:(c + 1) * P], ident[0:E, 0:E])
            last.then_inc(w_ps, 1)

            def transposes(h, s):
                pe.wait_ge(v_ready, h + 1)
                for c in range(NC):
                    last = pe.transpose(TA[:, c * P:(c + 1) * P], v[:, s, c * P:(c + 1) * P], ident)
                last.then_inc(vT_ps, 1)
                for c in range(NC):
                    last = pe.transpose(TB[:, c * P:(c + 1) * P], ct[:, s, c * P:(c + 1) * P], ident)
                last.then_inc(cT_ps, 1)
                pe.wait_ge(w_ready, h + 1)
                pe.wait_ge(skip_ready, h + 1)
                pe.matmul(DX[:, :], skip_b[:, s, :], w[:, s, :], start=True, stop=True).then_inc(dx_ps, 1)

            def conv(h, s, c, half):
                u = 2 * c + half
                if half == 0:
                    pe.wait_ge(kv_ready, h * NC + c + 1)
                    if c == 0:
                        pe.wait_ge(toep_lo, h + 1)
                if not (among(h, 0) and u < 4):
                    pe.wait_ge(z_done, h * 8 + u - 3)
                n = slice(half * 512, (half + 1) * 512)
                for a in range(c + 1):
                    high, low = (toep[:, s, part, (c - a) * P:(c - a + 1) * P] for part in range(2))
                    pe.matmul(Y[u % 4][:, :], high, kv[:, s, 0, a, n], start=(a == 0), stop=False)
                    pe.matmul(Y[u % 4][:, :], high, kv[:, s, 1, a, n], start=False, stop=False)
                    last = pe.matmul(Y[u % 4][:, :], low, kv[:, s, 0, a, n], start=False, stop=(a == c))
                last.then_inc(conv_done, 1)

            def turn_o(h, s):
                pe.wait_ge(o_done, h * 8 + 8)
                for c in range(NC):
                    last = pe.transpose(OT[:, c * P:(c + 1) * P], o[:, s, c, :], ident)
                last.then_inc(oT_ps, 1)

            def turn_xn(h, s):
                pe.wait_ge(xn_ready, h + 1)
                for c in range(NC):
                    last = pe.transpose(TA[:, c * P:(c + 1) * P], xn[:, s, c * P:(c + 1) * P], ident)
                last.then_inc(xT_ps, 1)

            def router(h, s):
                pe.wait_ge(xT_sb, h + 1)
                for c in range(NC):
                    last = pe.matmul(DX[:, 0:E], xT[:, s, c, :], gateT[:, c, :], start=(c == 0), stop=(c == NC - 1))
                last.then_inc(logit_ps, 1)

            def iteration(h, s):
                for c in range(2):
                    for half in range(2):
                        conv(h, s, c, half)
                if not among(h, 0):
                    turn_o(h - 1, 1 - s)
                if not among(h, NT - 1):
                    pe.wait_ge(vT_sb, h + 1)
                    pe.wait_ge(cT_sb, h + 1)
                    if not among(h, 0, 1):
                        pe.wait_ge(xT_sb, h - 1)
                        pe.wait_ge(sc_ready, h - 1)
                    transposes(h + 1, 1 - s)
                for half in range(2):
                    conv(h, s, 2, half)
                if not among(h, 0):
                    if not among(h, NT - 1):
                        pe.wait_ge(vT_sb, h + 2)
                    turn_xn(h - 1, 1 - s)
                conv(h, s, 3, 0)
                if not among(h, 0):
                    if not among(h, NT - 1):
                        pe.wait_ge(dc_ready, h + 2)
                    router(h - 1, 1 - s)
                conv(h, s, 3, 1)

            transposes(0, 0)
            pe.wait_ge(w_sb, 1)
            for h in range(3):
                iteration(h, h % 2)
            with pe.Fori(0, 13) as i:
                iteration(i * 2 + 3, 1)
                iteration(i * 2 + 4, 0)
            for h in range(NT - 3, NT):
                iteration(h, h % 2)
            turn_o(NT - 1, 1)

            pe.wait_ge(z_done, 8 * NT)
            for n in range(2 * NC + n_up):
                if n >= 4:
                    pe.wait_ge(w_sb, n - 2)
                    pe.wait_ge(sh_lo, n - 3)
                if n < 2 * NC:
                    c, g = n // 2, n % 2
                    pe.wait_ge(sh_gu_in, 32)
                    for a in range(n_up):
                        last = pe.transpose(Y[n % 4][:, a * P:(a + 1) * P],
                                            ring[:, g, a * L + c * P:a * L + (c + 1) * P], ident)
                else:
                    a = n - 2 * NC
                    pe.wait_ge(sh_down_in, 16)
                    for c in range(NC):
                        last = pe.transpose(Y[n % 4][:, c * P:(c + 1) * P],
                                            ring[:, 2, c * SI + a * P:c * SI + (a + 1) * P], ident)
                last.then_inc(w_ps, 1)
            turn_xn(NT - 1, 1)
            pe.wait_ge(sc_ready, NT - 1)
            router(NT - 1, 1)

            pe.wait_ge(w_sb, 1 + 2 * NC + n_up)
            pe.wait_ge(sh_lo, 2 * NC + n_up)
            pe.wait_ge(pre_ready, NT)
            pe.wait_ge(dve_setup, 6)
            for g in range(4):
                t8 = slice(8 * g, 8 * g + 8)
                pe.matmul(Y[g][:, :], sq16[:, 0, :], pre[:, t8, :], start=True, stop=False)
                pe.matmul(Y[g][:, :], sq16[:, 1, :], mask[:, t8, :], start=False, stop=False)
                pe.matmul(Y[g][:, :], sq16[:, 2, :], pre[:, NT:NT + 1, :].to_broadcast([P, 8, E]),
                          start=False, stop=True).then_inc(pos_ps, 1)

            def b_turn(t, s):
                pe.wait_ge(b_xn_in[s], landed(t, s, 16))
                for c in range(NC):
                    last = pe.transpose(TA[:, c * P:(c + 1) * P], xn[:, s, c * P:(c + 1) * P], ident)
                last.then_inc(b_xT_ps, 1)

            def b_half(t, s, g):
                for c in range(NC):
                    for a, b in ((0, 0), (0, 1), (1, 0)):
                        last = pe.matmul(Y[2 * s + g][:, 0:SI], xTs[:, s, a, c, :], sh_gu[:, b, c, g * SI:(g + 1) * SI],
                                         start=(c + a + b == 0), stop=(c == NC - 1 and a == 1))
                last.then_inc(up_ps if g else gate_ps, 1)

            def b_turn_hid(t, s):
                pe.wait_ge(b_hid, t + 1)
                if not among(t, 0):
                    pe.wait_ge(b_hT_lo, t)
                for a in range(n_up):
                    last = pe.transpose(TB[:, a * P:(a + 1) * P], hid[:, s, a * P:(a + 1) * P], ident)
                last.then_inc(b_hT_ps, 1)

            def b_out(t, s):
                pe.wait_ge(b_hT_lo, t + 1)
                for c in range(n_up):
                    for a, b in ((0, 0), (0, 1), (1, 0)):
                        last = pe.matmul(DN[s][:, :], hTs[:, s, a, c, :], sh_d[:, b, c, :],
                                         start=(c + a + b == 0), stop=(c == n_up - 1 and a == 1))
                last.then_inc(b_down, 1)

            def b_iteration(t, s, first=False, last=False):
                pe.wait_ge(b_xT_lo, t + 1)
                if not last:
                    b_turn(t + 1, 1 - s)
                if first:
                    pe.wait_ge(pos_sb, 4)
                elif not among(t, 1):
                    pe.wait_ge(b_hid, t - 1)
                b_half(t, s, 0)
                if not first:
                    b_turn_hid(t - 1, 1 - s)
                b_half(t, s, 1)
                if not first:
                    if among(t, 1):
                        pe.wait_ge(x1_ready, NT)
                        pe.wait_ge(sc_ready, NT)
                    elif not among(t, 2):
                        pe.wait_ge(y_ready, t - 2)
                    b_out(t - 1, 1 - s)

            b_turn(0, 0)
            b_iteration(0, 0, first=True)
            b_iteration(1, 1)
            b_iteration(2, 0)
            with pe.Fori(0, 14) as i:
                b_iteration(i * 2 + 3, 1)
                b_iteration(i * 2 + 4, 0)
            b_iteration(NT - 1, 1, last=True)
            b_turn_hid(NT - 1, 1)
            pe.wait_ge(y_ready, NT - 2)
            b_out(NT - 1, 1)

            def c_turn(e, s, r):
                pe.wait_ge(gathered[r], (e - r) * 4 + 16)
                for c in range(NC):
                    last = pe.transpose(TA[:, c * P:(c + 1) * P], xg[r][:, c * P:(c + 1) * P], ident)
                last.then_inc(c_xT_ps, 1)

            def c_up(e, s, r, part):
                for c in range(2 * part, 2 * part + 2):
                    last = pe.matmul(Y[s][:, 0:SI], xT[:, s, c, :], ring[:, r, c * SI:(c + 1) * SI],
                                     start=(c == 0), stop=(c == NC - 1))
                if part:
                    last.then_inc(c_gu, 1)

            def c_turn_hid(e, s):
                pe.wait_ge(c_hid, e + 1)
                for a in range(2):
                    last = pe.transpose(TB[0:IH, a * P:(a + 1) * P], hid[:, s, a * IH:(a + 1) * IH], ident)
                last.then_inc(c_hT_ps, 1)

            def c_out(e, s, r):
                pe.wait_ge(c_hT_sb, e + 1)
                for a in range(2):
                    o_w = NC * SI + a * L
                    last = pe.matmul(DN[s][:, :], hT[0:IH, s, a, :], ring[0:IH, r, o_w:o_w + L], start=(a == 0), stop=(a == 1))
                last.then_inc(c_down, 1)

            def c_iteration(e, s, r, first=False, last=False):
                pe.wait_ge(c_xT_sb, e + 1)
                if not last:
                    c_turn(e + 1, 1 - s, (r + 1) % 4)
                pe.wait_ge(weights_in[r], (e - r) * 8 + 32)
                if not (first or among(e, 1)):
                    pe.wait_ge(c_hid, e - 1)
                c_up(e, s, r, 0)
                if not first:
                    c_turn_hid(e - 1, 1 - s)
                c_up(e, s, r, 1)
                if not first:
                    if not among(e, 1, 2):
                        pe.wait_ge(eo_ready, e - 2)
                    c_out(e - 1, 1 - s, (r + NW - 1) % NW)

            pe.wait_ge(b_xT_lo, NT)
            c_turn(0, 0, 0)
            pe.wait_ge(y_ready, NT)
            for e in range(4):
                c_iteration(e, e % 2, e % NW, first=(e == 0))
            with pe.Fori(1, E // NW - 1) as i:
                for r in range(NW):
                    c_iteration(i * NW + r, r % 2, r)
            for e in range(E - NW, E):
                c_iteration(e, e % 2, e % NW, last=(e == E - 1))
            c_turn_hid(E - 1, 1)
            pe.wait_ge(eo_ready, E - 2)
            c_out(E - 1, 1, NW - 1)

        @block.scalar
        def _(act):
            act.wait_ge(small_in, 48)
            act.wait_ge(dve_setup, 3)
            act.activation(kpad[:, 0:L], z[0:NT, 0, ::-1], ACT.Copy).then_inc(krev_ready, 1)

            def sqrt1(h):
                act.wait_ge(ln1_mv, h + 1)
                act.activation(sd1[:], mv1[:, 1:2], ACT.Sqrt, bias=eps[:, 0:1]).then_inc(ln1_sd, 1)

            def apply1(h, s):
                act.wait_ge(ln1_nb, h + 1)
                if not among(h, 0, 1):
                    act.wait_ge(vT_ps, h - 1)
                    act.wait_ge(w_ready, h - 1)
                act.activation(v[:, s, :], xt[:, s, :], ACT.Identity, bias=nb1[:, 0:1], scale=rs1[:, 0:1]).then_inc(v_ready, 1)

            def filter_blocks(h, s):
                act.wait_ge(tile_in[s], landed(h, s, 64))
                if not among(h, 0, 1):
                    act.wait_ge(conv_done, h * 8 - 8)
                act.activation(toep[:, s, 0, :], gr[:, s, ::-1], ACT.Copy).then_inc(g_ready, 1)
                if not among(h, 0, 1):
                    act.wait_ge(dx_ps, h - 1)
                act.activation(skip_b[:, s, :], same_b, ACT.Copy, scale=skip_c[:, s, :]).then_inc(skip_ready, 1)

            def evacuate(h, s):
                act.wait_ge(vT_ps, h + 1)
                if not among(h, 0, 1):
                    act.wait_ge(kvp_ready, h * NC - NC)
                act.activation(vT[:, s, :, :].rearrange("p c n -> p (c n)"), TA[:, :], ACT.Copy).then_inc(vT_sb, 1)
                act.wait_ge(cT_ps, h + 1)
                if not among(h, 0, 1):
                    act.wait_ge(z_done, h * 8 - 8)
                act.activation(cT[:, s, :, :].rearrange("p c n -> p (c n)"), TB[:, :], ACT.Copy).then_inc(cT_sb, 1)

            def kv_high_part(h, s, c):
                act.wait_ge(kvp_ready, h * NC + c + 1)
                if not among(h, 0, 1) and c == 0:
                    act.wait_ge(conv_done, h * 8 - 8)
                act.activation(kv[:, s, 0, c, :], kvp[:, c % 2, :], ACT.Copy).then_inc(kv_high, 1)

            def sqrt2(h):
                act.wait_ge(ln2_mv, h + 1)
                act.activation(sd2[:], mv2[:, 1:2], ACT.Sqrt, bias=eps[:, 0:1]).then_inc(ln2_sd, 1)

            def apply2(h, s):
                act.wait_ge(ln2_nb, h + 1)
                if not among(h, 0, 1):
                    act.wait_ge(xn_out[s], landed(h - 2, s, 16))
                act.activation(xn[:, s, :], x1[:, s, :], ACT.Identity, bias=nb2[:, 0:1], scale=rs2[:, 0:1]).then_inc(xn_ready, 1)

            def evacuate_xn(h, s):
                act.wait_ge(xT_ps, h + 1)
                if not among(h, 0, 1):
                    act.wait_ge(logit_ps, h - 1)
                act.activation(xT[:, s, :, :].rearrange("p c n -> p (c n)"), TA[:, :], ACT.Copy).then_inc(xT_sb, 1)

            def keep_scores(h):
                act.wait_ge(sc_ready, h + 1)
                act.activation(sc_all[:, bass.ds(h, 1), :].rearrange("p a e -> p (a e)"), sc[:], ACT.Copy).then_inc(sc_kept, 1)
                act.wait_ge(s8_ready, h + 1)
                act.activation(s8_all[:, bass.ds(h, 1), :].rearrange("p a e -> p (a e)"), s8[:], ACT.Copy).then_inc(sc_kept, 1)

            def iteration(h, s):
                prev, nxt, nxt2 = not among(h, -1, 0), not among(h, NT - 1), not among(h, NT - 2, NT - 1)
                if not among(h, -1, 0, 1):
                    keep_scores(h - 2)
                if nxt:
                    filter_blocks(h + 1, 1 - s)
                    evacuate(h + 1, 1 - s)
                if prev:
                    sqrt2(h - 1)
                    apply2(h - 1, 1 - s)
                if nxt:
                    kv_high_part(h + 1, 1 - s, 0)
                    kv_high_part(h + 1, 1 - s, 1)
                if prev:
                    evacuate_xn(h - 1, 1 - s)
                if nxt2:
                    sqrt1(h + 2)
                if nxt:
                    kv_high_part(h + 1, 1 - s, 2)
                if nxt2:
                    apply1(h + 2, s)
                if nxt:
                    kv_high_part(h + 1, 1 - s, 3)

            sqrt1(0)
            apply1(0, 0)
            act.wait_ge(w_ps, 1)
            act.activation(gateT[:].rearrange("p c e -> p (c e)"), Y[0][:, 0:NC * E], ACT.Copy).then_inc(w_sb, 1)
            for h in range(-1, 3):
                iteration(h, h % 2)
            with act.Fori(0, 13) as i:
                iteration(i * 2 + 3, 1)
                iteration(i * 2 + 4, 0)
            for h in range(NT - 3, NT):
                iteration(h, h % 2)
            keep_scores(NT - 2)
            sqrt2(NT - 1)
            apply2(NT - 1, 1)
            for n in range(2 * NC + n_up):
                act.wait_ge(w_ps, n + 2)
                if n < 2 * NC:
                    c, g = n // 2, n % 2
                    act.activation(sh_gu[:, 0, c, g * SI:(g + 1) * SI], Y[n % 4][:, 0:SI], ACT.Copy).then_inc(w_sb, 1)
                else:
                    act.activation(sh_d[:, 0, n - 2 * NC, :], Y[n % 4][:, :], ACT.Copy).then_inc(w_sb, 1)
            evacuate_xn(NT - 1, 1)
            keep_scores(NT - 1)

            act.wait_ge(sc_kept, 2 * NT)
            act.activation(sc_all[:].rearrange("p t e -> p (t e)"), sc_all[:].rearrange("p t e -> p (t e)"), ACT.Exp).then_inc(exp_ready, 1)
            act.activation(s8_all[:].rearrange("p t e -> p (t e)"), s8_all[:].rearrange("p t e -> p (t e)"), ACT.Exp).then_inc(exp_ready, 1)
            act.wait_ge(o_done, 8 * NT)
            for g in range(4):
                act.wait_ge(pos_ps, g + 1)
                act.activation(pos[:, 8 * g:8 * g + 8, :].rearrange("p t e -> p (t e)"), Y[g][:, :], ACT.Copy).then_inc(pos_sb, 1)

            def b_evacuate(t, s):
                act.wait_ge(b_xT_ps, t + 1)
                if not among(t, 0, 1):
                    act.wait_ge(up_ps, t - 1)
                act.activation(xTs[:, s, 0, :, :].rearrange("p c n -> p (c n)"), TA[:, :], ACT.Copy).then_inc(b_xT_sb, 1)

            def b_gate(t, s):
                act.wait_ge(gate_ps, t + 1)
                if not among(t, 0, 1):
                    act.wait_ge(b_hid, t - 1)
                act.activation(sg[:, s, :], Y[2 * s][:, 0:SI], ACT.Silu).then_inc(b_silu, 1)

            def b_evacuate_hid(t, s):
                act.wait_ge(b_hT_ps, t + 1)
                if not among(t, 0, 1):
                    act.wait_ge(b_down, t - 1)
                act.activation(hTs[:, s, 0, :, :].rearrange("p c n -> p (c n)"), TB[:, 0:SI], ACT.Copy).then_inc(b_hT_sb, 1)

            def b_iteration(t, s):
                if not among(t, NT - 1):
                    b_evacuate(t + 1, 1 - s)
                b_gate(t, s)
                if not among(t, 0):
                    b_evacuate_hid(t - 1, 1 - s)

            b_evacuate(0, 0)
            for t in range(3):
                b_iteration(t, t % 2)
            with act.Fori(0, 14) as i:
                b_iteration(i * 2 + 3, 1)
                b_iteration(i * 2 + 4, 0)
            b_iteration(NT - 1, 1)
            b_evacuate_hid(NT - 1, 1)

            def c_evacuate(e, s, first=False):
                act.wait_ge(c_xT_ps, e + 1)
                if first:
                    act.wait_ge(up_ps, NT)
                else:
                    act.wait_ge(c_gu, e - 1)
                act.activation(xT[:, s, :, :].rearrange("p c n -> p (c n)"), TA[:, :], ACT.Copy).then_inc(c_xT_sb, 1)

            def c_gate(e, s):
                act.wait_ge(c_gu, e + 1)
                if among(e, 0):
                    act.wait_ge(b_hid, NT)
                elif not among(e, 1):
                    act.wait_ge(c_hid, e - 1)
                act.activation(sg[:, s, 0:I], Y[s][:, 0:I], ACT.Silu).then_inc(c_silu, 1)

            def c_evacuate_hid(e, s):
                act.wait_ge(c_hT_ps, e + 1)
                if among(e, 0):
                    act.wait_ge(b_down, NT)
                elif not among(e, 1):
                    act.wait_ge(c_down, e - 1)
                act.activation(hT[0:IH, s, 0:2, :].rearrange("p c n -> p (c n)"), TB[0:IH, 0:2 * P], ACT.Copy).then_inc(c_hT_sb, 1)

            def c_iteration(e, s, last=False):
                if not last:
                    c_evacuate(e + 1, 1 - s, first=(among(e, 0)))
                if not among(e, 0):
                    c_evacuate_hid(e - 1, 1 - s)
                c_gate(e, s)

            c_evacuate(0, 0, first=True)
            for e in range(3):
                c_iteration(e, e % 2)
            with act.Fori(0, (E - 4) // 2) as i:
                c_iteration(i * 2 + 3, 1)
                c_iteration(i * 2 + 4, 0)
            c_iteration(E - 1, 1, last=True)
            c_evacuate_hid(E - 1, 1)

        @block.gpsimd
        def _(pool):
            def product(h, s, c):
                if c == 0:
                    pool.wait_ge(vT_sb, h + 1)
                    pool.wait_ge(cT_sb, h + 1)
                if not (among(h, 0) and c < 2):
                    pool.wait_ge(kv_ready, h * NC + c - 1)
                a = vT[:, s, c, :].rearrange("p (b i) -> p b i", i=NH).unsqueeze(3).to_broadcast([P, B, NH, NH])
                d = cT[:, s, c, :].rearrange("p (b j) -> p b j", j=NH).unsqueeze(2).to_broadcast([P, B, NH, NH])
                pool.tensor_tensor(kvp[:, c % 2, :].rearrange("p (b i j) -> p b i j", i=NH, j=NH), a, d,
                                   ALU.mult).then_inc(kvp_ready, 1)

            def low_part(h, s, c):
                pool.wait_ge(kvp_ready, h * NC + c + 1)
                pool.wait_ge(kv_high, h * NC + c + 1)
                if not among(h, 0, 1) and c == 0:
                    pool.wait_ge(conv_done, h * 8 - 8)
                pool.tensor_tensor(kv[:, s, 1, c, :], kvp[:, c % 2, :], kv[:, s, 0, c, :].bitcast(F32),
                                   ALU.subtract).then_inc(kv_ready, 1)

            def v_ctx(h, s):
                pool.wait_ge(v_ready, h + 1)
                if not among(h, 0, 1):
                    pool.wait_ge(xr_ready, h - 1)
                pool.tensor_tensor(w[:, s, :], v[:, s, :], ct[:, s, :], ALU.mult).then_inc(w_ready, 1)

            def residual(h, s):
                pool.wait_ge(dc_ready, h + 1)
                if not among(h, 0, 1):
                    pool.wait_ge(x1_ready, h - 1)
                pool.tensor_tensor(xr[:, s, :], w[:, s, :], xt[:, s, :], ALU.add).then_inc(xr_ready, 1)

            def tile(h, s):
                product(h, s, 0)
                product(h, s, 1)
                low_part(h, s, 0)
                residual(h, s)
                product(h, s, 2)
                low_part(h, s, 1)
                if not among(h, NT - 1):
                    v_ctx(h + 1, 1 - s)
                product(h, s, 3)
                low_part(h, s, 2)
                low_part(h, s, 3)

            v_ctx(0, 0)
            for h in range(3):
                tile(h, h % 2)
            with pool.Fori(0, 14) as i:
                tile(i * 2 + 3, 1)
                tile(i * 2 + 4, 0)
            tile(NT - 1, 1)

            pool.wait_ge(pads_out, 48)

            def place(t, s):
                pool.wait_ge(slot_ready, t * 2 + 2)
                pool.sem_inc(pool_turn, 1)
                for c in range(K):
                    pool.indirect_dma_start(
                        out=table, out_offset=bass.IndirectOffsetOnAxis(ap=slot[:, s, c:c + 1], axis=0),
                        in_=recs[:, s, c, :], in_offset=None, bounds_check=CAP * E - 1, oob_is_err=False,
                    ).then_inc(placed[s], 16)

            with pool.Fori(0, NT // 2) as i:
                place(i * 2, 0)
                place(i * 2 + 1, 1)

            def fetch(e, r):
                pool.tensor_copy(idx_g[:, r:r + 1], idx_i[:, bass.ds(e, 1)]).then_inc(idx_g_ready, 1)
                pool.wait_ge(idx_g_ready, e + 1)
                if not among(e, 0, 1, 2, 3):
                    pool.wait_ge(c_xT_ps, e - 3)
                pool.sem_inc(pool_turn, 1)
                pool.indirect_dma_start(out=xg[r], out_offset=None, in_=xn_rows,
                                        in_offset=bass.IndirectOffsetOnAxis(ap=idx_g[:, r:r + 1], axis=0),
                                        ).then_inc(gathered[r], 16)

            def add(e, s, r):
                pool.tensor_copy(idx_a[:, r:r + 1], idx_i[:, bass.ds(e, 1)]).then_inc(idx_a_ready, 1)
                pool.wait_ge(idx_a_ready, e + 1)
                pool.wait_ge(eo_ready, e + 1)
                if not among(e, 0):
                    pool.wait_ge(added, e * 16)
                pool.sem_inc(pool_turn, 1)
                pool.indirect_dma_start(out=out, out_offset=bass.IndirectOffsetOnAxis(ap=idx_a[:, r:r + 1], axis=0),
                                        in_=y[:, s, :], in_offset=None, compute_op=ALU.add).then_inc(added, 16)

            pool.wait_ge(idx_i_ready, 1)
            for s in range(2):
                pool.wait_ge(xn_out[s], NT // 2 * 16)
            for e in range(3):
                fetch(e, e)
            for s in range(2):
                pool.wait_ge(y_out[s], NT // 2 * 16)
            for e in range(4):
                fetch(e + 3, (e + 3) % 4)
                add(e, e % 2, e)
            with pool.Fori(1, E // 4 - 1) as i:
                for n in range(4):
                    fetch(i * 4 + n + 3, (n + 3) % 4)
                    add(i * 4 + n, n % 2, n)
            for e in range(E - 4, E):
                if e + 3 < E:
                    fetch(e + 3, (e + 3) % 4)
                add(e, e % 2, e % 4)
            pool.wait_ge(added, E * 16)

        @block.vector
        def _(dve):
            dve.memset(zeros[:], 0.0).then_inc(dve_setup, 1)
            dve.memset(kpad[:], 0.0).then_inc(dve_setup, 1)
            dve.memset(eps[:], EPS).then_inc(dve_setup, 1)
            dve.memset(pre[:, 0, :], 0.0).then_inc(dve_setup, 1)
            dve.wait_ge(consts_in, 16)
            dve.tensor_copy(sq16[:].rearrange("p a n -> p (a n)"), sq[:, 1:4, :].rearrange("p a n -> p (a n)")).then_inc(dve_setup, 2)

            def moments(src, st, mv, n, stats, mean):
                dve.bn_stats(st[:], src).then_inc(stats, 1)
                dve.wait_ge(stats, n + 1)
                dve.sem_inc(dve_turn, 1)
                dve.bn_aggr(mv[:], st[:]).then_inc(mean, 1)

            def factors(mv, sd, rs, nb, n, root, rstd, ready):
                dve.wait_ge(root, n + 1)
                dve.reciprocal(rs[:], sd[:]).then_inc(rstd, 1)
                dve.wait_ge(rstd, n + 1)
                dve.tensor_scalar(nb[:], mv[:, 0:1], rs[:, 0:1], -1.0, ALU.mult, ALU.mult).then_inc(ready, 1)

            def moments1(h, s):
                dve.wait_ge(tile_in[s], landed(h, s, 64))
                if not among(h, 0):
                    dve.wait_ge(v_ready, h)
                moments(xt[:, s, :], st1, mv1, h, ln1_stats, ln1_mv)

            def factors1(h):
                factors(mv1, sd1, rs1, nb1, h, ln1_sd, ln1_rstd, ln1_nb)

            def factors2(h):
                factors(mv2, sd2, rs2, nb2, h, ln2_sd, ln2_rstd, ln2_nb)

            def filter_low(h, s):
                dve.wait_ge(g_ready, h + 1)
                dve.tensor_tensor(toep[:, s, 1, :], gr[:, s, ::-1], toep[:, s, 0, :].bitcast(F32), ALU.subtract).then_inc(toep_lo, 1)

            def sum_i(h, s, c):
                for half in range(2):
                    u = 2 * c + half
                    dve.wait_ge(conv_done, h * 8 + u + 1)
                    if not (among(h, 0) and u < 4):
                        dve.wait_ge(o_done, h * 8 + u - 3)
                    m = cT[:, s, c, half * 64:(half + 1) * 64].unsqueeze(2).to_broadcast([P, 64, NH])
                    dve.tensor_tensor(z[:, u % 4, :].rearrange("p (n j) -> p n j", j=NH),
                                      Y[u % 4][:, :].rearrange("p (n j) -> p n j", j=NH), m, ALU.mult).then_inc(z_done, 1)
                for half in range(2):
                    u = 2 * c + half
                    dve.wait_ge(z_done, h * 8 + u + 1)
                    dve.tensor_reduce(o[:, s, c, half * 64:(half + 1) * 64].rearrange("p (b j) -> p b j", j=NH),
                                      z[:, u % 4, :].rearrange("p (b i j) -> p b j i", i=NH, j=NH), AX.X, ALU.add).then_inc(o_done, 1)

            def skip_term(h, s):
                dve.wait_ge(dx_ps, h + 1)
                dve.tensor_tensor(w[:, s, :], DX[:, :], ct[:, s, :], ALU.mult).then_inc(dc_ready, 1)

            def finish_x1(h, s):
                dve.wait_ge(oT_ps, h + 1)
                dve.wait_ge(xr_ready, h + 1)
                if not among(h, 0):
                    dve.wait_ge(xn_ready, h)
                if not among(h, 0, 1):
                    dve.wait_ge(x1_out[s], landed(h - 2, s, 16))
                dve.tensor_tensor(x1[:, s, :], OT[:, :], xr[:, s, :], ALU.add).then_inc(x1_ready, 1)
                dve.wait_ge(x1_ready, h + 1)
                moments(x1[:, s, :], st2, mv2, h, ln2_stats, ln2_mv)

            def choose(h):
                dve.wait_ge(logit_ps, h + 1)
                dve.sem_inc(dve_turn, 1)
                dve.max(m8[:], DX[:, 0:E]).then_inc(max_ready, 1)
                dve.wait_ge(max_ready, h + 1)
                if not among(h, 0):
                    dve.wait_ge(sc_kept, h * 2)
                dve.tensor_scalar(sc[:], DX[:, 0:E], m8[:, 0:1], FLOOR, ALU.subtract, ALU.max).then_inc(sc_ready, 1)
                dve.wait_ge(sc_ready, h + 1)
                dve.sem_inc(dve_turn, 1)
                dve.max(s8[:], sc[:]).then_inc(s8_ready, 1)
                dve.wait_ge(s8_ready, h + 1)
                dve.sem_inc(dve_turn, 1)
                dve.max_index(i8[:], s8[:], sc[:]).then_inc(i8_ready, 1)
                dve.wait_ge(i8_ready, h + 1)
                idx = idx_all[:, bass.ds(h, 1), :].rearrange("p a k -> p (a k)")
                dve.tensor_copy(idx, i8[:, 0:K]).then_inc(idx_ready, 1)
                dve.wait_ge(idx_ready, h + 1)
                dve.tensor_tensor(chosen[:], iota[:].unsqueeze(1).to_broadcast([P, K, E]), idx.unsqueeze(2).to_broadcast([P, K, E]),
                                  ALU.is_equal).then_inc(onehot_ready, 1)
                dve.wait_ge(onehot_ready, h + 1)
                mk = mask[:, bass.ds(h, 1), :].rearrange("p a e -> p (a e)")
                dve.tensor_reduce(mk, chosen[:].rearrange("p k e -> p e k"), AX.X, ALU.max).then_inc(mask_ready, 1)
                dve.wait_ge(mask_ready, h + 1)
                dve.tensor_tensor(pre[:, bass.ds(h + 1, 1), :], pre[:, bass.ds(h, 1), :], mask[:, bass.ds(h, 1), :],
                                  ALU.add).then_inc(pre_ready, 1)

            def iteration(h, s):
                sum_i(h, s, 0)
                sum_i(h, s, 1)
                if not among(h, 0):
                    finish_x1(h - 1, 1 - s)
                if not among(h, NT - 1):
                    skip_term(h + 1, 1 - s)
                if not among(h, 0):
                    factors2(h - 1)
                if not among(h, NT - 1):
                    filter_low(h + 1, 1 - s)
                sum_i(h, s, 2)
                if not among(h, NT - 2, NT - 1):
                    moments1(h + 2, s)
                    factors1(h + 2)
                sum_i(h, s, 3)
                if not among(h, 0):
                    choose(h - 1)

            dve.wait_ge(small_in, 48)
            for h in range(2):
                moments1(h, h)
                factors1(h)
                if h == 0:
                    filter_low(0, 0)
                    skip_term(0, 0)
            for h in range(3):
                iteration(h, h % 2)
            with dve.Fori(0, 13) as i:
                iteration(i * 2 + 3, 1)
                iteration(i * 2 + 4, 0)
            for h in range(NT - 3, NT):
                iteration(h, h % 2)
            finish_x1(NT - 1, 1)
            factors2(NT - 1)
            for n in range(2 * NC + n_up):
                dve.wait_ge(w_sb, n + 2)
                if n < 2 * NC:
                    c, g = n // 2, n % 2
                    part, bank = sh_gu[:, :, c, g * SI:(g + 1) * SI], Y[n % 4][:, 0:SI]
                else:
                    part, bank = sh_d[:, :, n - 2 * NC, :], Y[n % 4][:, :]
                dve.tensor_tensor(part[:, 1, :], bank, part[:, 0, :].bitcast(F32), ALU.subtract).then_inc(sh_lo, 1)
            choose(NT - 1)

            dve.wait_ge(exp_ready, 2)
            dve.tensor_reduce(sums[:], sc_all[:], AX.X, ALU.add).then_inc(sums_ready, 1)
            dve.wait_ge(sums_ready, 1)
            dve.reciprocal(rinv[:], sums[:]).then_inc(rinv_ready, 1)
            dve.wait_ge(rinv_ready, 1)
            dve.tensor_tensor(rec[:, :, :, 1], s8_all[:, :, 0:K], rinv[:].unsqueeze(2).to_broadcast([P, NT, K]),
                              ALU.mult).then_inc(rec_ready, 1)
            dve.wait_ge(rec_ready, 1)
            dve.wait_ge(pos_sb, 4)

            def place(t, s, first=False):
                idx = idx_all[:, bass.ds(t, 1), :].rearrange("p a k -> p (a k)")
                dve.tensor_tensor(onehot, iota[:].unsqueeze(1).to_broadcast([P, K, E]), idx.unsqueeze(2).to_broadcast([P, K, E]),
                                  ALU.is_equal).then_inc(b_onehot, 1)
                dve.wait_ge(b_onehot, t + 1)
                dve.tensor_tensor(prod, onehot,
                                  pos[:, bass.ds(t, 1), :].to_broadcast([P, K, E]), ALU.mult).then_inc(prod_ready, 1)
                dve.wait_ge(prod_ready, t + 1)
                dve.tensor_reduce(pk[:], prod, AX.X, ALU.add).then_inc(pk_ready, 1)
                dve.wait_ge(pk_ready, t + 1)
                if not first:
                    dve.wait_ge(placed[s], landed(t - 2, s, K * 16))
                dve.scalar_tensor_tensor(slot[:, s, :], pk[:], float(E), idx_all[:, bass.ds(t, 1), :].rearrange("p a k -> p (a k)"),
                                         ALU.mult, ALU.add).then_inc(slot_ready, 1)
                dve.tensor_copy(recs[:, s, :, :].rearrange("p k c -> p (k c)"),
                                rec[:, bass.ds(t, 1), :, :].rearrange("p a k c -> p (a k c)")).then_inc(slot_ready, 1)

            def b_rows_low(t, s):
                dve.wait_ge(b_xT_sb, t + 1)
                dve.tensor_tensor(xTs[:, s, 1, :, :].rearrange("p c n -> p (c n)"), TA[:, :],
                                  xTs[:, s, 0, :, :].rearrange("p c n -> p (c n)").bitcast(F32), ALU.subtract).then_inc(b_xT_lo, 1)

            def b_hidden_low(t, s):
                dve.wait_ge(b_hT_sb, t + 1)
                dve.tensor_tensor(hTs[:, s, 1, :, :].rearrange("p c n -> p (c n)"), TB[:, 0:SI],
                                  hTs[:, s, 0, :, :].rearrange("p c n -> p (c n)").bitcast(F32), ALU.subtract).then_inc(b_hT_lo, 1)

            def b_hidden(t, s):
                dve.wait_ge(b_silu, t + 1)
                dve.wait_ge(up_ps, t + 1)
                if not among(t, 0, 1):
                    dve.wait_ge(b_hT_ps, t - 1)
                dve.tensor_tensor(hid[:, s, :], Y[2 * s + 1][:, 0:SI], sg[:, s, :], ALU.mult).then_inc(b_hid, 1)

            def b_result(t, s):
                dve.wait_ge(b_down, t + 1)
                dve.wait_ge(b_x1_in[s], landed(t, s, 16))
                if not among(t, 0, 1):
                    dve.wait_ge(y_out[s], landed(t - 2, s, 16))
                dve.tensor_tensor(y[:, s, :], DN[s][:, :], xr[:, s, :], ALU.add).then_inc(y_ready, 1)

            def b_iteration(t, s):
                if not among(t, NT - 1):
                    b_rows_low(t + 1, 1 - s)
                place(t, s, first=among(t, 0, 1))
                if not among(t, 0):
                    b_hidden_low(t - 1, 1 - s)
                b_hidden(t, s)
                if not among(t, 0):
                    b_result(t - 1, 1 - s)

            b_rows_low(0, 0)
            for t in range(3):
                b_iteration(t, t % 2)
            with dve.Fori(0, 14) as i:
                b_iteration(i * 2 + 3, 1)
                b_iteration(i * 2 + 4, 0)
            b_iteration(NT - 1, 1)
            b_hidden_low(NT - 1, 1)
            b_result(NT - 1, 1)

            dve.wait_ge(table_in, 16)
            dve.tensor_copy(idx_i[:], tbl[:, :, 0]).then_inc(idx_i_ready, 1)

            def c_hidden(e, s):
                dve.wait_ge(c_silu, e + 1)
                if among(e, 0):
                    dve.wait_ge(b_hT_ps, NT)
                elif not among(e, 1):
                    dve.wait_ge(c_hT_ps, e - 1)
                dve.tensor_tensor(hid[:, s, 0:I], Y[s][:, I:2 * I], sg[:, s, 0:I], ALU.mult).then_inc(c_hid, 1)

            def c_result(e, s):
                dve.wait_ge(c_down, e + 1)
                if among(e, 0, 1):
                    dve.wait_ge(y_out[s], NT // 2 * 16)
                else:
                    dve.wait_ge(added, e * 16 - 16)
                dve.tensor_scalar(y[:, s, :], DN[s][:, :], tbl[:, bass.ds(e, 1), 1], None, ALU.mult).then_inc(eo_ready, 1)

            def c_iteration(e, s):
                c_hidden(e, s)
                if not among(e, 0):
                    c_result(e - 1, 1 - s)

            for e in range(4):
                c_iteration(e, e % 2)
            with dve.Fori(2, E // 2) as i:
                c_iteration(i * 2, 0)
                c_iteration(i * 2 + 1, 1)
            c_result(E - 1, 1)


_INS = ['x', 'fside_S2_0', 'ctx_2048', 'L0_xattn_k', 'L0_ffn_gate_w', 'L0_ffn_gate_up_proj', 'L0_ffn_down_proj',
        'L0_ffn_shared_gate_w', 'L0_ffn_shared_up_w', 'L0_ffn_shared_down_w']


def constants():
    p = np.arange(P)
    b, j = p // NH, p % NH
    sq = np.stack([np.eye(P), b[:, None] == b[None], (b[:, None] == b[None]) & (j[:, None] < j[None]),
                   b[:, None] < b[None]], 1).astype(np.float32)
    iota = np.tile(np.arange(E, dtype=np.float32), (P, 1))
    rec = np.zeros((P, NT, K, 2), np.float32)
    rec[..., 0] = (b * D + j)[:, None, None] + NH * np.arange(NT)[None, :, None]
    table = np.zeros((CAP, E, 2), np.float32)
    table[..., 0] = T + np.arange(CAP)[:, None]
    return {"sq": sq, "iota": iota, "rec": rec.reshape(P, -1), "table": table.reshape(CAP * E, 2)}


def kernel(**inputs):
    import numpy as _np
    import concourse.bacc as _bacc
    from concourse import mybir as _mybir
    from concourse.bass_utils import run_bass_kernel_spmd as _run

    nc = _bacc.Bacc("TRN2", target_bir_lowering=False, num_devices=1)
    arrays, args = {}, []
    data = [(name, inputs[name]) for name in _INS] + list(constants().items())
    for name, value in data:
        a = _np.ascontiguousarray(value)
        arrays[f"in_{name}_dram"] = a
        args.append(nc.dram_tensor(f"in_{name}_dram", a.shape, _mybir.dt.from_np(a.dtype), kind="ExternalInput").ap())
    args.append(nc.dram_tensor("out_0_dram", (T + CAP, L), _mybir.dt.float32, kind="ExternalOutput").ap())
    build(nc, *args)
    r = _run(nc, [arrays], core_ids=[0])
    return r.results[0]["out_0_dram"][:T].reshape(B, D, L)
```

```python
from contextlib import ExitStack

import numpy as np

import concourse.bass as bass
from concourse import mybir

F32 = mybir.dt.float32
F32R = mybir.dt.float32r
BF16 = mybir.dt.bfloat16
I32 = mybir.dt.int32
U32 = mybir.dt.uint32
ALU = mybir.AluOpType
ACT = mybir.ActivationFunctionType
AX = mybir.AxisListType

P = 128
B, D, L = 16, 256, 512
NH = 8
NT = D // NH
T = B * D
NC = L // P
E, K, CAP = 64, 6, 128
I = 192
SI = 2 * I
IH = I // 2
KVC = B * NH * NH
EPS = 1e-5
FLOOR = -87.3
OTHER, MARK = 1.0, 2.0
NW = 4
NG = 8
NY = 4
NP = 4


def build(nc, x, skip, ctx_in, k, gate_w, gate_up, down, sh_gate, sh_up, sh_down,
          c_sq, c_iota, c_rec, c_table, out):
    xn_rows = nc.dram_tensor("xn_rows", [T + CAP, L], F32, kind="Internal").ap()
    x1_rows = nc.dram_tensor("x1_rows", [T, L], F32, kind="Internal").ap()
    krev = nc.dram_tensor("krev", [NT, L + P], F32, kind="Internal").ap()
    table = nc.dram_tensor("table", [CAP * E, 2], F32, kind="Internal").ap()

    with ExitStack() as stack:
        def sb(name, shape, dt=F32):
            return stack.enter_context(nc.sbuf_tensor(name, shape, dt))

        def ps(name):
            return stack.enter_context(nc.psum_tensor(name, [P, 512], F32))

        def sem(name):
            return stack.enter_context(nc.semaphore(name))

        sq = sb("sq", [P, 4, P])
        ident, same_b = sq[:, 0, :], sq[:, 1, :]
        sq16 = sb("sq16", [P, 3, P], BF16)
        iota = sb("iota", [P, E])
        eps = sb("eps", [P, 1])
        zeros = sb("zeros", [P, L])
        kpad = sb("kpad", [NT, L + P])
        gate_in = sb("gate_in", [E, L])
        gateT = sb("gateT", [P, NC, E])
        ring = sb("ring", [P, NW, NC * SI + 2 * L])
        xt = sb("xt", [P, 2, L])
        ct = sb("ct", [P, 2, L])
        gr = sb("gr", [P, 2, L])
        toep = sb("toep", [P, 2, 2, L], F32R)
        skip_c = sb("skip_c", [P, 2, 1])
        v = sb("v", [P, 2, L])
        w = sb("w", [P, 2, L])
        skip_b = sb("skip_b", [P, 2, P])
        vT = sb("vT", [P, 2, NC, P])
        cT = sb("cT", [P, 2, NC, P])
        split = sb("split", [P, 2 * 2 * NC * KVC], F32R)
        kv = split[:].rearrange("p (s a c n) -> p s a c n", s=2, a=2, c=NC)
        kvp = [ring[:, 3, 0:KVC], ring[:, 3, KVC:2 * KVC],
               ring[:, 0, SI * NC:], ring[:, 1, SI * NC:]]
        z = sb("z", [P, 4, 512])
        kin = z[0:NT, 0, :]
        o = sb("o", [P, 2, NC, P])
        xr = sb("xr", [P, 2, L])
        x1 = sb("x1", [P, 2, L])
        xn = sb("xn", [P, 2, L])
        xT = sb("xT", [P, 2, NC, P])
        mean1, var1, sd1, rs1, nb1 = sb("mean1", [P, 1]), sb("var1", [P, 1]), sb("sd1", [P, 1]), sb("rs1", [P, 1]), sb("nb1", [P, 1])
        st2, mv2, sd2, rs2, nb2 = sb("st2", [P, 6]), sb("mv2", [P, 2]), sb("sd2", [P, 1]), sb("rs2", [P, 1]), sb("nb2", [P, 1])
        m8 = sb("m8", [P, 8])
        sc = sb("sc", [P, E + 2])
        s6 = sb("s6", [P, 8])
        marked = sb("marked", [P, E + 2])
        s8 = sb("s8", [P, 8])
        i8 = sb("i8", [P, 8], U32)
        sc_all = sb("sc_all", [P, NT, E])
        s8_all = sb("s8_all", [P, NT, 8])
        idx_all = sb("idx_all", [P, NT, K])
        mask = sb("mask", [P, NT, E], BF16)
        pre = sb("pre", [P, NT + 1, E], BF16)
        sums, rinv = sb("sums", [P, NT]), sb("rinv", [P, NT])
        rec = sb("rec", [P, NT, K, 2])
        pk = sb("pk", [P, K])
        slot = sb("slot", [P, NP, K], I32)
        recs = sb("recs", [P, NP, K, 2])
        tbl = sb("tbl", [P, E, 2])
        idx_i = sb("idx_i", [P, E], I32)
        idx_g, idx_a = sb("idx_g", [P, NG], I32), sb("idx_a", [P, NY], I32)
        n_gu, n_d = NC * 2 * SI, SI // P * L
        sh_gu = split[:, 0:2 * n_gu].rearrange("p (a c n) -> p a c n", a=2, c=NC)
        sh_d = split[:, 2 * n_gu:2 * (n_gu + n_d)].rearrange("p (a c n) -> p a c n", a=2, c=SI // P)
        at = 2 * (n_gu + n_d)
        xTs = split[:, at:at + 4 * L].rearrange("p (s a c n) -> p s a c n", s=2, a=2, c=NC)
        hTs = split[:, at + 4 * L:at + 4 * L + 4 * SI].rearrange("p (s a c n) -> p s a c n", s=2, a=2, c=SI // P)
        c_d = split[0:IH, 0:8 * L].rearrange("p (s a c n) -> p s a c n", s=2, a=2, c=2)
        sg = vT[:].rearrange("p s c n -> p s (c n)")[:, :, 0:SI]
        hid = cT[:].rearrange("p s c n -> p s (c n)")[:, :, 0:SI]
        y = o[:].rearrange("p s c n -> p s (c n)")
        pos = z[:].rearrange("p s (t e) -> p (s t) e", e=E)
        prod = w[:, 0, 0:K * E].rearrange("p (k e) -> p k e", e=E)
        onehot = w[:, 1, 0:K * E].rearrange("p (k e) -> p k e", e=E)
        xg = [buf[:, s, :] for buf in (xt, ct, v, x1) for s in range(2)]
        eo = [y[:, 0, :], y[:, 1, :], w[:, 0, :], w[:, 1, :]]

        Y = [ps(f"Y{n}") for n in range(4)]
        TA, TB, OT, DX = ps("TA"), ps("TB"), ps("OT"), ps("DX")
        DN = [OT, DX]

        k_in, consts_in, small_in = sem("k_in"), sem("consts_in"), sem("small_in")
        gate_w_in, sh_gu_in, sh_down_in = sem("gate_w_in"), sem("sh_gu_in"), sem("sh_down_in")
        dve_setup, krev_ready, krev_out, pads_out = sem("dve_setup"), sem("krev_ready"), sem("krev_out"), sem("pads_out")
        dve_turn, pool_turn = sem("dve_turn"), sem("pool_turn")
        w_ps, w_sb = sem("w_ps"), sem("w_sb")
        tile_in, filter_in = [sem("tile_in0"), sem("tile_in1")], [sem("filter_in0"), sem("filter_in1")]
        ln1_mean, ln1_var, ln1_sd, ln1_rstd = sem("ln1_mean"), sem("ln1_var"), sem("ln1_sd"), sem("ln1_rstd")
        ln1_nb, ln2_nb, toep_lo, kvp_ready, kv_high = sem("ln1_nb"), sem("ln2_nb"), sem("toep_lo"), sem("kvp_ready"), sem("kv_high")
        skip_ready = sem("skip_ready")
        b_xT_lo, b_hT_lo, sh_lo = sem("b_xT_lo"), sem("b_hT_lo"), sem("sh_lo")
        v_ready, w_ready, g_ready = sem("v_ready"), sem("w_ready"), sem("g_ready")
        vT_ps, cT_ps, dx_ps, vT_sb, cT_sb = sem("vT_ps"), sem("cT_ps"), sem("dx_ps"), sem("vT_sb"), sem("cT_sb")
        kv_ready, kv_last, conv_done, z_done, o_done = sem("kv_ready"), sem("kv_last"), sem("conv_done"), sem("z_done"), sem("o_done")
        dc_ready, xr_ready, oT_ps, x1_ready = sem("dc_ready"), sem("xr_ready"), sem("oT_ps"), sem("x1_ready")
        ln2_stats, ln2_mv, ln2_sd, ln2_rstd = sem("ln2_stats"), sem("ln2_mv"), sem("ln2_sd"), sem("ln2_rstd")
        xn_ready, xT_ps, xT_sb, logit_ps = sem("xn_ready"), sem("xT_ps"), sem("xT_sb"), sem("logit_ps")
        x1_out, xn_out = [sem("x1_out0"), sem("x1_out1")], [sem("xn_out0"), sem("xn_out1")]
        max_ready, sc_ready, s8_ready, i8_ready = sem("max_ready"), sem("sc_ready"), sem("s8_ready"), sem("i8_ready")
        sc_kept, idx_ready, s6_ready, b_onehot = sem("sc_kept"), sem("idx_ready"), sem("s6_ready"), sem("b_onehot")
        sc_setup, marked_ready = sem("sc_setup"), sem("marked_ready")
        mask_ready, pre_ready = sem("mask_ready"), sem("pre_ready")
        pos_ps, pos_sb, exp_ready = sem("pos_ps"), sem("pos_sb"), sem("exp_ready")
        sums_ready, rinv_ready, rec_ready = sem("sums_ready"), sem("rinv_ready"), sem("rec_ready")
        prod_ready, pk_ready, slot_ready = sem("prod_ready"), sem("pk_ready"), sem("slot_ready")
        placed = [sem(f"placed{r}") for r in range(NP)]
        b_xn_in, b_x1_in = [sem("b_xn_in0"), sem("b_xn_in1")], [sem("b_x1_in0"), sem("b_x1_in1")]
        b_xT_ps, b_xT_sb, gate_ps, up_ps = sem("b_xT_ps"), sem("b_xT_sb"), sem("gate_ps"), sem("up_ps")
        b_silu, b_hid, b_hT_ps, b_hT_sb, b_down = sem("b_silu"), sem("b_hid"), sem("b_hT_ps"), sem("b_hT_sb"), sem("b_down")
        y_ready, y_out = sem("y_ready"), [sem("y_out0"), sem("y_out1")]
        table_in, idx_i_ready, idx_g_ready, idx_a_ready = sem("table_in"), sem("idx_i_ready"), sem("idx_g_ready"), sem("idx_a_ready")
        weights_in = [sem(f"weights_in{r}") for r in range(NW)]
        gathered = [sem(f"gathered{r}") for r in range(NG)]
        c_xT_ps, c_xT_sb, c_gu, c_silu = sem("c_xT_ps"), sem("c_xT_sb"), sem("c_gu"), sem("c_silu")
        c_hid, c_hT_ps, c_hT_sb, c_down = sem("c_hid"), sem("c_hT_ps"), sem("c_hT_sb"), sem("c_down")
        c_hT_lo, c_d_high, c_d_low = sem("c_hT_lo"), sem("c_d_high"), sem("c_d_low")
        eo_ready, added = sem("eo_ready"), sem("added")

        def rows(dram, h):
            return dram.rearrange("(b h i) l -> h b i l", b=B, i=NH)[h]

        def landed(n, s, each):
            return (n - s) * (each // 2) + each

        def among(n, *numbers):
            return isinstance(n, int) and n in numbers

        x_f = x.rearrange("b d l -> (b d) l")
        c_f = ctx_in.rearrange("b d l -> (b d) l")
        skip_v = skip.rearrange("(h i) -> h i", i=NH)
        n_up = SI // P

        def weights(sp, e, r):
            sp.dma_start(ring[:, r, 0:NC * SI].rearrange("p (c n) -> p c n", c=NC),
                         gate_up[e].rearrange("(c p) n -> p c n", p=P)).then_inc(weights_in[r], 16)
            sp.dma_start(ring[0:IH, r, NC * SI:].rearrange("p (c n) -> p c n", c=2),
                         down[e].rearrange("(c p) n -> p c n", p=IH)).then_inc(weights_in[r], 16)

        turn_bank = [TB, DX, TB, TB, Y[0], Y[1], TB, Y[2], Y[3], TB, Y[3]]
        n_turn = 2 * NC + n_up

        def shared_part(n):
            if n < 2 * NC:
                c, g = n // 2, n % 2
                return sh_gu[:, :, c, g * SI:(g + 1) * SI], turn_bank[n][:, 0:SI]
            return sh_d[:, :, n - 2 * NC, :], turn_bank[n][:, :]

        block = stack.enter_context(nc.Block())

        @block.sync
        def _(sp):
            def load_rows(h, s):
                sp.dma_start(xt[:, s, :], rows(x_f, h)).then_inc(tile_in[s], 16)
                sp.dma_start(ct[:, s, :], rows(c_f, h)).then_inc(tile_in[s], 16)

            def load_filter(h, s):
                win = krev[h, 0:L]
                sp.dma_start(gr[:, s, :], bass.AP(win.tensor, win.offset, [[1, P], [1, L]])).then_inc(filter_in[s], 16)
                row = skip_v[h]
                sp.dma_start(skip_c[:, s, :], bass.AP(row.tensor, row.offset, [[0, B], [1, NH], [1, 1]])).then_inc(filter_in[s], 16)

            sp.dma_start(kin, k).then_inc(k_in, 16)
            load_rows(0, 0)
            sp.dma_start(sq[:], c_sq).then_inc(consts_in, 16)
            sp.dma_start(gate_in[:], gate_w).then_inc(gate_w_in, 16)
            sp.wait_ge(dve_setup, 1)
            sp.wait_ge(krev_ready, 1)
            sp.dma_start(krev, kpad[:]).then_inc(krev_out, 16)
            load_rows(1, 1)
            sp.dma_start(iota[:], c_iota).then_inc(small_in, 16)
            sp.wait_ge(krev_out, 16)
            load_filter(0, 0)
            load_filter(1, 1)
            sp.dma_start(rec[:].rearrange("p t k c -> p (t k c)"), c_rec).then_inc(small_in, 16)
            sp.wait_ge(dve_setup, 3)
            sp.dma_start(table, c_table).then_inc(pads_out, 16)
            sp.dma_start(xn_rows[T:T + CAP, :], zeros[:]).then_inc(pads_out, 16)
            sp.dma_start(out[T:T + CAP, :], zeros[:]).then_inc(pads_out, 16)
            sp.dma_start(ring[:, 0, 0:n_up * L].rearrange("p (a l) -> p a l", a=n_up),
                         sh_gate.rearrange("(a p) l -> p a l", p=P)).then_inc(sh_gu_in, 16)
            sp.dma_start(ring[:, 1, 0:n_up * L].rearrange("p (a l) -> p a l", a=n_up),
                         sh_up.rearrange("(a p) l -> p a l", p=P)).then_inc(sh_gu_in, 16)
            sp.dma_start(ring[:, 2, 0:NC * SI].rearrange("p (a i) -> p a i", a=NC),
                         sh_down.rearrange("(a p) i -> p a i", p=P)).then_inc(sh_down_in, 16)

            def store(h, s):
                sp.wait_ge(x1_ready, h + 1)
                sp.dma_start(rows(x1_rows, h), x1[:, s, :]).then_inc(x1_out[s], 16)
                sp.wait_ge(xn_ready, h + 1)
                sp.dma_start(rows(xn_rows[0:T, :], h), xn[:, s, :]).then_inc(xn_out[s], 16)

            def iteration(h, s):
                if not among(h, NT - 3, NT - 2, NT - 1):
                    sp.wait_ge(xr_ready, h + 2)
                    sp.wait_ge(toep_lo, h + 2)
                    load_rows(h + 3, 1 - s)
                    load_filter(h + 3, 1 - s)
                if not among(h, 0):
                    store(h - 1, 1 - s)

            sp.wait_ge(xr_ready, 1)
            sp.wait_ge(toep_lo, 1)
            load_rows(2, 0)
            load_filter(2, 0)
            iteration(0, 0)
            iteration(1, 1)
            iteration(2, 0)
            with sp.Fori(0, 13) as i:
                iteration(i * 2 + 3, 1)
                iteration(i * 2 + 4, 0)
            for h in range(NT - 3, NT):
                iteration(h, h % 2)

            def b_load_xn(t, s):
                if among(t, 0, 1):
                    sp.wait_ge(xT_ps, NT - 1 + t)
                    sp.wait_ge(xn_out[s], NT // 2 * 16)
                else:
                    sp.wait_ge(b_xT_ps, t - 1)
                sp.dma_start(xn[:, s, :], rows(xn_rows[0:T, :], t)).then_inc(b_xn_in[s], 16)

            def b_load_x1(t, s):
                sp.wait_ge(x1_out[s], landed(t, s, 16))
                sp.dma_start(xr[:, s, :], rows(x1_rows, t)).then_inc(b_x1_in[s], 16)

            def b_store(t, s):
                sp.wait_ge(y_ready, t + 1)
                sp.dma_start(rows(out[0:T, :], t), y[:, s, :]).then_inc(y_out[s], 16)

            b_load_xn(0, 0)
            store(NT - 1, 1)
            b_load_xn(1, 1)
            for t in range(2):
                b_load_x1(t, t)

            def b_iteration(t, s, fetch_xn=True, fetch_x1=True, expert=None):
                if fetch_xn:
                    b_load_xn(t + 2, s)
                if expert is not None:
                    weights(sp, expert, expert)
                if not among(t, 0):
                    b_store(t - 1, 1 - s)
                    if fetch_x1:
                        b_load_x1(t + 1, 1 - s)

            b_iteration(0, 0)
            b_iteration(1, 1)
            sp.wait_ge(sh_lo, n_turn)
            for t in range(2, 2 + NW):
                b_iteration(t, t % 2, expert=t - 2)
            with sp.Fori((2 + NW) // 2, NT // 2 - 1) as i:
                b_iteration(i * 2, 0)
                b_iteration(i * 2 + 1, 1)
            b_iteration(NT - 2, 0, fetch_xn=False)
            b_iteration(NT - 1, 1, fetch_xn=False, fetch_x1=False)
            b_store(NT - 1, 1)

            with sp.Fori(0, E // NW - 1) as i:
                for r in range(NW):
                    sp.wait_ge(c_down, i * NW + r + 1)
                    weights(sp, i * NW + r + NW, r)

        @block.tensor
        def _(pe):
            pe.wait_ge(consts_in, 16)
            pe.wait_ge(gate_w_in, 16)
            for c in range(NC):
                last = pe.transpose(Y[0][:, c * E:(c + 1) * E], gate_in[:, c * P:(c + 1) * P], ident[0:E, 0:E])
            last.then_inc(w_ps, 1)

            def transposes(h, s):
                pe.wait_ge(v_ready, h + 1)
                for c in range(NC):
                    last = pe.transpose(TA[:, c * P:(c + 1) * P], v[:, s, c * P:(c + 1) * P], ident)
                last.then_inc(vT_ps, 1)
                for c in range(NC):
                    last = pe.transpose(TB[:, c * P:(c + 1) * P], ct[:, s, c * P:(c + 1) * P], ident)
                last.then_inc(cT_ps, 1)
                pe.wait_ge(w_ready, h + 1)
                pe.wait_ge(skip_ready, h + 1)
                pe.matmul(DX[:, :], skip_b[:, s, :], w[:, s, :], start=True, stop=True).then_inc(dx_ps, 1)

            def conv(h, s, c, half):
                u = 2 * c + half
                if half == 0:
                    if c < NC - 1:
                        pe.wait_ge(kv_ready, h * (NC - 1) + c + 1)
                    else:
                        pe.wait_ge(kv_last, h + 1)
                    if c == 0:
                        pe.wait_ge(toep_lo, h + 1)
                if not (among(h, 0) and u < 4):
                    pe.wait_ge(z_done, h * 8 + u - 3)
                n = slice(half * 512, (half + 1) * 512)
                for a in range(c + 1):
                    high, low = (toep[:, s, part, (c - a) * P:(c - a + 1) * P] for part in range(2))
                    pe.matmul(Y[u % 4][:, :], high, kv[:, s, 0, a, n], start=(a == 0), stop=False)
                    pe.matmul(Y[u % 4][:, :], high, kv[:, s, 1, a, n], start=False, stop=False)
                    last = pe.matmul(Y[u % 4][:, :], low, kv[:, s, 0, a, n], start=False, stop=(a == c))
                last.then_inc(conv_done, 1)

            def turn_o(h, s):
                pe.wait_ge(o_done, h * 8 + 8)
                for c in range(NC):
                    last = pe.transpose(OT[:, c * P:(c + 1) * P], o[:, s, c, :], ident)
                last.then_inc(oT_ps, 1)

            def turn_xn(h, s):
                pe.wait_ge(xn_ready, h + 1)
                for c in range(NC):
                    last = pe.transpose(TA[:, c * P:(c + 1) * P], xn[:, s, c * P:(c + 1) * P], ident)
                last.then_inc(xT_ps, 1)

            def router(h, s):
                pe.wait_ge(xT_sb, h + 1)
                for c in range(NC):
                    last = pe.matmul(DX[:, 0:E], xT[:, s, c, :], gateT[:, c, :], start=(c == 0), stop=(c == NC - 1))
                last.then_inc(logit_ps, 1)

            def turn_weights(n):
                if n == 0:
                    pe.wait_ge(cT_sb, NT)
                elif n == 1:
                    pe.wait_ge(sc_ready, NT - 2)
                    pe.wait_ge(dc_ready, NT)
                elif n in (4, 5, 7, 8):
                    pe.wait_ge(z_done, 8 * (NT - 1) + {4: 5, 5: 6, 7: 7, 8: 8}[n])
                else:
                    pe.wait_ge(sh_lo, {2: 0, 3: 2, 6: 3, 9: 6, 10: 8}[n] + 1)
                if n < 2 * NC:
                    c, g = n // 2, n % 2
                    pe.wait_ge(sh_gu_in, 32)
                    for a in range(n_up):
                        last = pe.transpose(turn_bank[n][:, a * P:(a + 1) * P],
                                            ring[:, g, a * L + c * P:a * L + (c + 1) * P], ident)
                else:
                    a = n - 2 * NC
                    pe.wait_ge(sh_down_in, 16)
                    for c in range(NC):
                        last = pe.transpose(turn_bank[n][:, c * P:(c + 1) * P],
                                            ring[:, 2, c * SI + a * P:c * SI + (a + 1) * P], ident)
                last.then_inc(w_ps, 1)

            def iteration(h, s):
                conv(h, s, 0, 0)
                conv(h, s, 0, 1)
                conv(h, s, 1, 0)
                if not among(h, 0):
                    turn_o(h - 1, 1 - s)
                if among(h, NT - 1):
                    turn_weights(0)
                conv(h, s, 1, 1)
                if among(h, NT - 1):
                    turn_weights(1)
                if not among(h, NT - 1):
                    pe.wait_ge(vT_sb, h + 1)
                    pe.wait_ge(cT_sb, h + 1)
                    if not among(h, 0, 1):
                        pe.wait_ge(xT_sb, h - 1)
                        pe.wait_ge(sc_ready, h - 1)
                    transposes(h + 1, 1 - s)
                for half in range(2):
                    conv(h, s, 2, half)
                if among(h, NT - 1):
                    turn_weights(2)
                if not among(h, 0):
                    if not among(h, NT - 1):
                        pe.wait_ge(vT_sb, h + 2)
                    turn_xn(h - 1, 1 - s)
                conv(h, s, 3, 0)
                if among(h, NT - 1):
                    turn_weights(3)
                if not among(h, 0):
                    if not among(h, NT - 1):
                        pe.wait_ge(dc_ready, h + 2)
                    else:
                        pe.wait_ge(sh_lo, 2)
                    router(h - 1, 1 - s)
                conv(h, s, 3, 1)

            transposes(0, 0)
            pe.wait_ge(w_sb, 1)
            for h in range(3):
                iteration(h, h % 2)
            with pe.Fori(0, 13) as i:
                iteration(i * 2 + 3, 1)
                iteration(i * 2 + 4, 0)
            for h in range(NT - 3, NT):
                iteration(h, h % 2)

            def places(g):
                if g == 0:
                    pe.wait_ge(pre_ready, NT)
                    pe.wait_ge(dve_setup, 6)
                    pe.wait_ge(x1_ready, NT)
                    pe.wait_ge(sc_ready, NT)
                elif g >= 2:
                    pe.wait_ge(pos_sb, g - 1)
                t8 = slice(8 * g, 8 * g + 8)
                pe.matmul(DN[g % 2][:, :], sq16[:, 0, :], pre[:, t8, :], start=True, stop=False)
                pe.matmul(DN[g % 2][:, :], sq16[:, 1, :], mask[:, t8, :], start=False, stop=False)
                pe.matmul(DN[g % 2][:, :], sq16[:, 2, :], pre[:, NT:NT + 1, :].to_broadcast([P, 8, E]),
                          start=False, stop=True).then_inc(pos_ps, 1)

            def b_turn(t, s):
                pe.wait_ge(b_xn_in[s], landed(t, s, 16))
                for c in range(NC):
                    last = pe.transpose(TA[:, c * P:(c + 1) * P], xn[:, s, c * P:(c + 1) * P], ident)
                last.then_inc(b_xT_ps, 1)

            def b_half(t, s, g):
                for c in range(NC):
                    for a, b in ((0, 0), (0, 1), (1, 0)):
                        last = pe.matmul(Y[2 * s + g][:, 0:SI], xTs[:, s, a, c, :], sh_gu[:, b, c, g * SI:(g + 1) * SI],
                                         start=(c + a + b == 0), stop=(c == NC - 1 and a == 1))
                last.then_inc(up_ps if g else gate_ps, 1)

            def b_turn_hid(t, s):
                pe.wait_ge(b_hid, t + 1)
                if not among(t, 0):
                    pe.wait_ge(b_hT_lo, t)
                for a in range(n_up):
                    last = pe.transpose(TB[:, a * P:(a + 1) * P], hid[:, s, a * P:(a + 1) * P], ident)
                last.then_inc(b_hT_ps, 1)

            def b_out(t, s):
                pe.wait_ge(b_hT_lo, t + 1)
                for c in range(n_up):
                    for a, b in ((0, 0), (0, 1), (1, 0)):
                        last = pe.matmul(DN[s][:, :], hTs[:, s, a, c, :], sh_d[:, b, c, :],
                                         start=(c + a + b == 0), stop=(c == n_up - 1 and a == 1))
                last.then_inc(b_down, 1)

            def b_iteration(t, s, last=False):
                pe.wait_ge(b_xT_lo, t + 1)
                if not last:
                    b_turn(t + 1, 1 - s)
                pe.wait_ge(b_hid, t - 1)
                b_half(t, s, 0)
                b_turn_hid(t - 1, 1 - s)
                b_half(t, s, 1)
                if among(t, 2):
                    pe.wait_ge(pos_sb, 4)
                else:
                    pe.wait_ge(y_ready, t - 2)
                b_out(t - 1, 1 - s)

            for n in range(4, 7):
                turn_weights(n)
            pe.wait_ge(xT_sb, NT - 1)
            b_turn(0, 0)
            turn_weights(7)
            turn_o(NT - 1, 1)
            turn_weights(8)
            pe.wait_ge(b_xT_lo, 1)
            pe.wait_ge(sh_lo, 2 * NC)
            b_half(0, 0, 0)
            turn_xn(NT - 1, 1)
            b_half(0, 0, 1)
            pe.wait_ge(sc_ready, NT - 1)
            router(NT - 1, 1)
            b_turn(1, 1)
            turn_weights(9)
            turn_weights(10)
            places(0)
            places(1)
            pe.wait_ge(b_xT_lo, 2)
            b_turn(2, 0)
            b_half(1, 1, 0)
            places(2)
            b_turn_hid(0, 0)
            pe.wait_ge(sh_lo, n_turn)
            b_half(1, 1, 1)
            places(3)
            pe.wait_ge(pos_sb, 3)
            b_out(0, 0)
            b_iteration(2, 0)
            with pe.Fori(0, 14) as i:
                b_iteration(i * 2 + 3, 1)
                b_iteration(i * 2 + 4, 0)
            b_iteration(NT - 1, 1, last=True)
            b_turn_hid(NT - 1, 1)
            pe.wait_ge(y_ready, NT - 2)
            b_out(NT - 1, 1)

            def c_turn(e, s, g):
                pe.wait_ge(gathered[g], (e - g) * (16 // NG) + 16)
                for c in range(NC):
                    last = pe.transpose(TA[:, c * P:(c + 1) * P], xg[g][:, c * P:(c + 1) * P], ident)
                last.then_inc(c_xT_ps, 1)

            def c_up(e, s, r, part):
                for c in range(2 * part, 2 * part + 2):
                    last = pe.matmul(Y[s][:, 0:SI], xT[:, s, c, :], ring[:, r, c * SI:(c + 1) * SI],
                                     start=(c == 0), stop=(c == NC - 1))
                if part:
                    last.then_inc(c_gu, 1)

            def c_turn_hid(e, s):
                pe.wait_ge(c_hid, e + 1)
                for a in range(2):
                    last = pe.transpose(TB[0:IH, a * P:(a + 1) * P], hid[:, s, a * IH:(a + 1) * IH], ident)
                last.then_inc(c_hT_ps, 1)

            def c_out(e, s):
                pe.wait_ge(c_d_low, e + 1)
                pe.wait_ge(c_hT_lo, e + 1)
                for c in range(2):
                    for a, b in ((0, 0), (0, 1), (1, 0)):
                        last = pe.matmul(DN[s][:, :], hTs[0:IH, s, a, c, :], c_d[:, s, b, c, :],
                                         start=(c + a + b == 0), stop=(c == 1 and a == 1))
                last.then_inc(c_down, 1)

            def c_iteration(e, g, first=False, last=False):
                s, r = g % 2, g % NW
                pe.wait_ge(c_xT_sb, e + 1)
                if not last:
                    c_turn(e + 1, 1 - s, (g + 1) % NG)
                pe.wait_ge(weights_in[r], (e - r) * 8 + 32)
                if not (first or among(e, 1)):
                    pe.wait_ge(c_hid, e - 1)
                c_up(e, s, r, 0)
                if not first:
                    c_turn_hid(e - 1, 1 - s)
                c_up(e, s, r, 1)
                if not first:
                    if not among(e, 1, 2):
                        pe.wait_ge(eo_ready, e - 2)
                    c_out(e - 1, 1 - s)

            pe.wait_ge(b_xT_lo, NT)
            c_turn(0, 0, 0)
            pe.wait_ge(y_ready, NT)
            for e in range(NG):
                c_iteration(e, e, first=(e == 0))
            with pe.Fori(1, E // NG - 1) as i:
                for g in range(NG):
                    c_iteration(i * NG + g, g)
            for e in range(E - NG, E):
                c_iteration(e, e % NG, last=(e == E - 1))
            c_turn_hid(E - 1, 1)
            pe.wait_ge(eo_ready, E - 2)
            c_out(E - 1, 1)

        @block.scalar
        def _(act):
            act.wait_ge(k_in, 16)
            act.activation(kpad[:, 0:L], z[0:NT, 0, ::-1], ACT.Copy).then_inc(krev_ready, 1)

            def minus_mean1(h, s):
                act.wait_ge(tile_in[s], landed(h, s, 32))
                if not among(h, 0):
                    act.wait_ge(ln1_nb, h)
                if not among(h, 0, 1):
                    act.wait_ge(vT_ps, h - 1)
                    act.wait_ge(w_ready, h - 1)
                act.activation(v[:, s, :], xt[:, s, :], ACT.Copy, scale=-1.0 / L, accum_out=mean1[:]).then_inc(ln1_mean, 1)

            def squares1(h, s):
                act.wait_ge(ln1_mean, h + 1)
                act.activation(v[:, s, :], xt[:, s, :], ACT.Square, bias=mean1[:, 0:1], accum_out=var1[:]).then_inc(ln1_var, 1)

            def sqrt1(h):
                act.wait_ge(ln1_var, h + 1)
                if not among(h, 0):
                    act.wait_ge(ln1_rstd, h)
                act.activation(sd1[:], var1[:], ACT.Sqrt, bias=eps[:, 0:1], scale=1.0 / L).then_inc(ln1_sd, 1)

            def apply1(h, s):
                act.wait_ge(ln1_nb, h + 1)
                act.activation(v[:, s, :], xt[:, s, :], ACT.Identity, bias=nb1[:, 0:1], scale=rs1[:, 0:1]).then_inc(v_ready, 1)

            def filter_blocks(h, s):
                act.wait_ge(filter_in[s], landed(h, s, 32))
                if not among(h, 0, 1):
                    act.wait_ge(conv_done, h * 8 - 8)
                act.activation(toep[:, s, 0, :], gr[:, s, ::-1], ACT.Copy).then_inc(g_ready, 1)
                if not among(h, 0, 1):
                    act.wait_ge(dx_ps, h - 1)
                act.activation(skip_b[:, s, :], same_b, ACT.Copy, scale=skip_c[:, s, :]).then_inc(skip_ready, 1)

            def evacuate(h, s):
                act.wait_ge(vT_ps, h + 1)
                if not among(h, 0, 1):
                    act.wait_ge(kvp_ready, h * NC - NC)
                act.activation(vT[:, s, :, :].rearrange("p c n -> p (c n)"), TA[:, :], ACT.Copy).then_inc(vT_sb, 1)
                act.wait_ge(cT_ps, h + 1)
                if not among(h, 0, 1):
                    act.wait_ge(z_done, h * 8 - 8)
                act.activation(cT[:, s, :, :].rearrange("p c n -> p (c n)"), TB[:, :], ACT.Copy).then_inc(cT_sb, 1)

            def kv_high_part(h, s, c):
                act.wait_ge(kvp_ready, h * NC + c + 1)
                if not among(h, 0, 1) and c == 0:
                    act.wait_ge(conv_done, h * 8 - 8)
                act.activation(kv[:, s, 0, c, :], kvp[c], ACT.Copy).then_inc(kv_high, 1)

            def sqrt2(h):
                act.wait_ge(ln2_mv, h + 1)
                act.activation(sd2[:], mv2[:, 1:2], ACT.Sqrt, bias=eps[:, 0:1]).then_inc(ln2_sd, 1)

            def apply2(h, s):
                act.wait_ge(ln2_nb, h + 1)
                if not among(h, 0, 1):
                    act.wait_ge(xn_out[s], landed(h - 2, s, 16))
                act.activation(xn[:, s, :], x1[:, s, :], ACT.Identity, bias=nb2[:, 0:1], scale=rs2[:, 0:1]).then_inc(xn_ready, 1)

            def evacuate_xn(h, s):
                act.wait_ge(xT_ps, h + 1)
                if not among(h, 0, 1):
                    act.wait_ge(logit_ps, h - 1)
                act.activation(xT[:, s, :, :].rearrange("p c n -> p (c n)"), TA[:, :], ACT.Copy).then_inc(xT_sb, 1)

            def keep_scores(h):
                act.wait_ge(sc_ready, h + 1)
                act.activation(sc_all[:, bass.ds(h, 1), :].rearrange("p a e -> p (a e)"), sc[:, 0:E], ACT.Copy).then_inc(sc_kept, 1)
                act.wait_ge(s8_ready, h + 1)
                act.activation(s8_all[:, bass.ds(h, 1), :].rearrange("p a e -> p (a e)"), s8[:], ACT.Copy).then_inc(sc_kept, 1)

            def shared_high(n):
                part, bank = shared_part(n)
                act.wait_ge(w_ps, n + 2)
                if n == 0:
                    act.wait_ge(conv_done, 8 * (NT - 1))
                if n == 2 * NC:
                    act.wait_ge(conv_done, 8 * NT)
                act.activation(part[:, 0, :], bank, ACT.Copy).then_inc(w_sb, 1)

            def iteration(h, s):
                prev, nxt, nxt2 = not among(h, -1, 0), not among(h, NT - 1), not among(h, NT - 2, NT - 1)
                if nxt:
                    filter_blocks(h + 1, 1 - s)
                if not among(h, -1, 0, 1):
                    keep_scores(h - 2)
                if nxt:
                    evacuate(h + 1, 1 - s)
                else:
                    shared_high(0)
                if prev:
                    sqrt2(h - 1)
                    apply2(h - 1, 1 - s)
                if not nxt:
                    for n in range(1, 3):
                        shared_high(n)
                if nxt:
                    kv_high_part(h + 1, 1 - s, 0)
                if nxt2:
                    minus_mean1(h + 2, s)
                if nxt:
                    kv_high_part(h + 1, 1 - s, 1)
                if nxt2:
                    squares1(h + 2, s)
                if prev:
                    evacuate_xn(h - 1, 1 - s)
                if nxt2:
                    sqrt1(h + 2)
                if nxt:
                    kv_high_part(h + 1, 1 - s, 2)
                if nxt2:
                    apply1(h + 2, s)
                if nxt:
                    kv_high_part(h + 1, 1 - s, 3)

            act.wait_ge(dve_setup, 3)
            minus_mean1(0, 0)
            squares1(0, 0)
            sqrt1(0)
            apply1(0, 0)
            act.wait_ge(w_ps, 1)
            act.activation(gateT[:].rearrange("p c e -> p (c e)"), Y[0][:, 0:NC * E], ACT.Copy).then_inc(w_sb, 1)
            for h in range(-1, 3):
                iteration(h, h % 2)
            with act.Fori(0, 13) as i:
                iteration(i * 2 + 3, 1)
                iteration(i * 2 + 4, 0)
            for h in range(NT - 3, NT):
                iteration(h, h % 2)
            def b_evacuate(t, s):
                act.wait_ge(b_xT_ps, t + 1)
                if not among(t, 0, 1):
                    act.wait_ge(up_ps, t - 1)
                act.activation(xTs[:, s, 0, :, :].rearrange("p c n -> p (c n)"), TA[:, :], ACT.Copy).then_inc(b_xT_sb, 1)

            def b_gate(t, s):
                act.wait_ge(gate_ps, t + 1)
                if not among(t, 0, 1):
                    act.wait_ge(b_hid, t - 1)
                act.activation(sg[:, s, :], Y[2 * s][:, 0:SI], ACT.Silu).then_inc(b_silu, 1)

            def b_evacuate_hid(t, s):
                act.wait_ge(b_hT_ps, t + 1)
                if not among(t, 0, 1):
                    act.wait_ge(b_down, t - 1)
                act.activation(hTs[:, s, 0, :, :].rearrange("p c n -> p (c n)"), TB[:, 0:SI], ACT.Copy).then_inc(b_hT_sb, 1)

            def b_iteration(t, s):
                if not among(t, NT - 1):
                    b_evacuate(t + 1, 1 - s)
                b_gate(t, s)
                if not among(t, 0):
                    b_evacuate_hid(t - 1, 1 - s)

            def places_out(g):
                act.wait_ge(pos_ps, g + 1)
                act.activation(pos[:, 8 * g:8 * g + 8, :].rearrange("p t e -> p (t e)"), DN[g % 2][:, :], ACT.Copy).then_inc(pos_sb, 1)

            for n in range(3, 7):
                shared_high(n)
            act.wait_ge(conv_done, 8 * NT)
            b_evacuate(0, 0)
            shared_high(7)
            sqrt2(NT - 1)
            apply2(NT - 1, 1)
            keep_scores(NT - 2)
            shared_high(8)
            evacuate_xn(NT - 1, 1)
            act.wait_ge(sc_kept, 2 * NT - 2)
            most, last = sc_all[:, 0:NT - 1, :], sc_all[:, NT - 1:NT, :]
            act.activation(most, most, ACT.Exp).then_inc(exp_ready, 1)
            b_evacuate(1, 1)
            shared_high(9)
            keep_scores(NT - 1)
            act.wait_ge(sc_kept, 2 * NT)
            act.activation(last, last, ACT.Exp).then_inc(exp_ready, 1)
            act.activation(s8_all[:].rearrange("p t e -> p (t e)"), s8_all[:].rearrange("p t e -> p (t e)"), ACT.Exp).then_inc(exp_ready, 1)
            act.wait_ge(o_done, 8 * NT)
            places_out(0)
            b_gate(0, 0)
            shared_high(10)
            places_out(1)
            b_evacuate(2, 0)
            b_evacuate_hid(0, 0)
            places_out(2)
            b_gate(1, 1)
            places_out(3)
            b_iteration(2, 0)
            with act.Fori(0, 14) as i:
                b_iteration(i * 2 + 3, 1)
                b_iteration(i * 2 + 4, 0)
            b_iteration(NT - 1, 1)
            b_evacuate_hid(NT - 1, 1)

            def c_evacuate(e, s, first=False):
                act.wait_ge(c_xT_ps, e + 1)
                if first:
                    act.wait_ge(up_ps, NT)
                else:
                    act.wait_ge(c_gu, e - 1)
                act.activation(xT[:, s, :, :].rearrange("p c n -> p (c n)"), TA[:, :], ACT.Copy).then_inc(c_xT_sb, 1)

            def c_gate(e, s):
                act.wait_ge(c_gu, e + 1)
                if among(e, 0):
                    act.wait_ge(b_hid, NT)
                elif not among(e, 1):
                    act.wait_ge(c_hid, e - 1)
                act.activation(sg[:, s, 0:I], Y[s][:, 0:I], ACT.Silu).then_inc(c_silu, 1)

            def c_evacuate_hid(e, s):
                act.wait_ge(c_hT_ps, e + 1)
                if among(e, 0):
                    act.wait_ge(b_down, NT)
                elif not among(e, 1):
                    act.wait_ge(c_down, e - 1)
                act.activation(hTs[0:IH, s, 0, 0:2, :].rearrange("p c n -> p (c n)"), TB[0:IH, 0:2 * P], ACT.Copy).then_inc(c_hT_sb, 1)

            def c_down_high(e, r):
                s = r % 2
                act.wait_ge(weights_in[r], (e - r) * 8 + 32)
                if not among(e, 0, 1):
                    act.wait_ge(c_down, e - 1)
                act.activation(c_d[:, s, 0, :, :].rearrange("p c n -> p (c n)"), ring[0:IH, r, NC * SI:], ACT.Copy).then_inc(c_d_high, 1)

            def c_iteration(e, r, last=False):
                s = r % 2
                if not last:
                    c_evacuate(e + 1, 1 - s, first=(among(e, 0)))
                if not among(e, 0):
                    c_evacuate_hid(e - 1, 1 - s)
                c_gate(e, s)
                c_down_high(e, r)

            c_evacuate(0, 0, first=True)
            for e in range(NW):
                c_iteration(e, e)
            with act.Fori(1, E // NW - 1) as i:
                for r in range(NW):
                    c_iteration(i * NW + r, r)
            for e in range(E - NW, E):
                c_iteration(e, e % NW, last=(e == E - 1))
            c_evacuate_hid(E - 1, 1)

        @block.gpsimd
        def _(pool):
            def product(h, s, c):
                if c == 0:
                    pool.wait_ge(vT_sb, h + 1)
                    pool.wait_ge(cT_sb, h + 1)
                if c < NC - 1 and not among(h, 0):
                    pool.wait_ge(kv_ready, (h - 1) * (NC - 1) + c + 1)
                elif not among(h, 0):
                    pool.wait_ge(kv_last, h)
                a = vT[:, s, c, :].rearrange("p (b i) -> p b i", i=NH).unsqueeze(3).to_broadcast([P, B, NH, NH])
                d = cT[:, s, c, :].rearrange("p (b j) -> p b j", j=NH).unsqueeze(2).to_broadcast([P, B, NH, NH])
                pool.tensor_tensor(kvp[c].rearrange("p (b i j) -> p b i j", i=NH, j=NH), a, d,
                                   ALU.mult).then_inc(kvp_ready, 1)

            def low_part(h, s, c):
                pool.wait_ge(kvp_ready, h * NC + c + 1)
                pool.wait_ge(kv_high, h * NC + c + 1)
                if not among(h, 0, 1) and c == 0:
                    pool.wait_ge(conv_done, h * 8 - 8)
                pool.tensor_tensor(kv[:, s, 1, c, :], kvp[c], kv[:, s, 0, c, :].bitcast(F32),
                                   ALU.subtract).then_inc(kv_ready, 1)

            def v_ctx(h, s):
                pool.wait_ge(v_ready, h + 1)
                if not among(h, 0, 1):
                    pool.wait_ge(xr_ready, h - 1)
                pool.tensor_tensor(w[:, s, :], v[:, s, :], ct[:, s, :], ALU.mult).then_inc(w_ready, 1)

            def tile(h, s):
                product(h, s, 0)
                product(h, s, 1)
                low_part(h, s, 0)
                product(h, s, 2)
                low_part(h, s, 1)
                product(h, s, 3)
                if not among(h, NT - 1):
                    v_ctx(h + 1, 1 - s)
                low_part(h, s, 2)

            v_ctx(0, 0)
            for h in range(3):
                tile(h, h % 2)
            with pool.Fori(0, 14) as i:
                tile(i * 2 + 3, 1)
                tile(i * 2 + 4, 0)
            tile(NT - 1, 1)

            pool.wait_ge(pads_out, 48)

            def scatter(t, r):
                pool.wait_ge(slot_ready, t * 2 + 2)
                pool.sem_inc(pool_turn, 1)
                for c in range(K):
                    pool.indirect_dma_start(
                        out=table, out_offset=bass.IndirectOffsetOnAxis(ap=slot[:, r, c:c + 1], axis=0),
                        in_=recs[:, r, c, :], in_offset=None, bounds_check=CAP * E - 1, oob_is_err=False,
                    ).then_inc(placed[r], 16)

            with pool.Fori(0, NT // NP) as i:
                for r in range(NP):
                    scatter(i * NP + r, r)

            def fetch(e, r):
                pool.tensor_copy(idx_g[:, r:r + 1], idx_i[:, bass.ds(e, 1)]).then_inc(idx_g_ready, 1)
                pool.wait_ge(idx_g_ready, e + 1)
                if not among(e, *range(NG)):
                    pool.wait_ge(c_xT_ps, e - NG + 1)
                pool.sem_inc(pool_turn, 1)
                pool.indirect_dma_start(out=xg[r], out_offset=None, in_=xn_rows,
                                        in_offset=bass.IndirectOffsetOnAxis(ap=idx_g[:, r:r + 1], axis=0),
                                        ).then_inc(gathered[r], 16)

            def add(e, r):
                pool.tensor_copy(idx_a[:, r:r + 1], idx_i[:, bass.ds(e, 1)]).then_inc(idx_a_ready, 1)
                pool.wait_ge(idx_a_ready, e + 1)
                pool.wait_ge(eo_ready, e + 1)
                if not among(e, 0):
                    pool.wait_ge(added, e * 16)
                pool.sem_inc(pool_turn, 1)
                pool.indirect_dma_start(out=out, out_offset=bass.IndirectOffsetOnAxis(ap=idx_a[:, r:r + 1], axis=0),
                                        in_=eo[r], in_offset=None, compute_op=ALU.add).then_inc(added, 16)

            for r in range(NP):
                pool.wait_ge(placed[r], NT // NP * K * 16)
            pool.dma_start(tbl[:].rearrange("p e c -> p (e c)"),
                           table.rearrange("(p e) c -> p (e c)", e=E)).then_inc(table_in, 16)
            pool.wait_ge(table_in, 16)
            pool.tensor_copy(idx_i[:], tbl[:, :, 0]).then_inc(idx_i_ready, 1)
            pool.wait_ge(idx_i_ready, 1)
            for s in range(2):
                pool.wait_ge(xn_out[s], NT // 2 * 16)
            for e in range(NG - 1):
                fetch(e, e)
            for s in range(2):
                pool.wait_ge(y_out[s], NT // 2 * 16)
            for e in range(NG):
                fetch(e + NG - 1, (e + NG - 1) % NG)
                add(e, e % NY)
            with pool.Fori(1, E // NG - 1) as i:
                for n in range(NG):
                    fetch(i * NG + n + NG - 1, (n + NG - 1) % NG)
                    add(i * NG + n, n % NY)
            for e in range(E - NG, E):
                if e + NG - 1 < E:
                    fetch(e + NG - 1, (e + NG - 1) % NG)
                add(e, e % NY)
            pool.wait_ge(added, E * 16)

        @block.vector
        def _(dve):
            dve.memset(kpad[:, L:], 0.0).then_inc(dve_setup, 1)
            dve.memset(eps[:], EPS).then_inc(dve_setup, 1)
            dve.memset(zeros[:], 0.0).then_inc(dve_setup, 1)
            dve.memset(pre[:, 0, :], 0.0).then_inc(dve_setup, 1)
            dve.memset(sc[:, E:], OTHER).then_inc(sc_setup, 1)
            dve.memset(s6[:, K:], OTHER).then_inc(sc_setup, 1)
            dve.wait_ge(consts_in, 16)
            dve.tensor_copy(sq16[:].rearrange("p a n -> p (a n)"), sq[:, 1:4, :].rearrange("p a n -> p (a n)")).then_inc(dve_setup, 2)

            def rstd1(h):
                dve.wait_ge(ln1_sd, h + 1)
                if not among(h, 0):
                    dve.wait_ge(v_ready, h)
                dve.reciprocal(rs1[:], sd1[:]).then_inc(ln1_rstd, 1)

            def shift1(h):
                dve.wait_ge(ln1_rstd, h + 1)
                dve.tensor_scalar(nb1[:], mean1[:, 0:1], rs1[:, 0:1], None, ALU.mult).then_inc(ln1_nb, 1)

            def stats2(h, s):
                dve.wait_ge(x1_ready, h + 1)
                dve.bn_stats(st2[:], x1[:, s, :]).then_inc(ln2_stats, 1)

            def mean2(h):
                dve.wait_ge(ln2_stats, h + 1)
                if not among(h, 0):
                    dve.wait_ge(xn_ready, h)
                dve.sem_inc(dve_turn, 1)
                dve.bn_aggr(mv2[:], st2[:]).then_inc(ln2_mv, 1)

            def rstd2(h):
                dve.wait_ge(ln2_sd, h + 1)
                dve.reciprocal(rs2[:], sd2[:]).then_inc(ln2_rstd, 1)

            def shift2(h):
                dve.wait_ge(ln2_rstd, h + 1)
                dve.tensor_scalar(nb2[:], mv2[:, 0:1], rs2[:, 0:1], -1.0, ALU.mult, ALU.mult).then_inc(ln2_nb, 1)

            def filter_low(h, s):
                dve.wait_ge(g_ready, h + 1)
                dve.tensor_tensor(toep[:, s, 1, :], gr[:, s, ::-1], toep[:, s, 0, :].bitcast(F32), ALU.subtract).then_inc(toep_lo, 1)

            def times(h, s, u):
                dve.wait_ge(conv_done, h * 8 + u + 1)
                if not (among(h, 0) and u < 4):
                    dve.wait_ge(o_done, h * 8 + u - 3)
                m = cT[:, s, u // 2, u % 2 * 64:(u % 2 + 1) * 64].unsqueeze(2).to_broadcast([P, 64, NH])
                dve.tensor_tensor(z[:, u % 4, :].rearrange("p (n j) -> p n j", j=NH),
                                  Y[u % 4][:, :].rearrange("p (n j) -> p n j", j=NH), m, ALU.mult).then_inc(z_done, 1)

            def total(h, s, u):
                dve.wait_ge(z_done, h * 8 + u + 1)
                dve.tensor_reduce(o[:, s, u // 2, u % 2 * 64:(u % 2 + 1) * 64].rearrange("p (b j) -> p b j", j=NH),
                                  z[:, u % 4, :].rearrange("p (b i j) -> p b j i", i=NH, j=NH), AX.X, ALU.add).then_inc(o_done, 1)

            def last_low_part(h, s):
                c = NC - 1
                dve.wait_ge(kv_high, h * NC + c + 1)
                if not among(h, 0, 1):
                    dve.wait_ge(conv_done, h * 8 - 8)
                dve.tensor_tensor(kv[:, s, 1, c, :], kvp[c], kv[:, s, 0, c, :].bitcast(F32),
                                  ALU.subtract).then_inc(kv_last, 1)

            def skip_term(h, s):
                dve.wait_ge(dx_ps, h + 1)
                dve.tensor_tensor(w[:, s, :], DX[:, :], ct[:, s, :], ALU.mult).then_inc(dc_ready, 1)

            def residual(h, s):
                dve.wait_ge(dc_ready, h + 1)
                if not among(h, 0, 1):
                    dve.wait_ge(x1_ready, h - 1)
                dve.tensor_tensor(xr[:, s, :], w[:, s, :], xt[:, s, :], ALU.add).then_inc(xr_ready, 1)

            def add_x1(h, s):
                dve.wait_ge(oT_ps, h + 1)
                dve.wait_ge(xr_ready, h + 1)
                if not among(h, 0, 1):
                    dve.wait_ge(x1_out[s], landed(h - 2, s, 16))
                dve.tensor_tensor(x1[:, s, :], OT[:, :], xr[:, s, :], ALU.add).then_inc(x1_ready, 1)

            def best_logit(h):
                dve.wait_ge(logit_ps, h + 1)
                dve.sem_inc(dve_turn, 1)
                dve.max(m8[:], DX[:, 0:E]).then_inc(max_ready, 1)

            def scores(h):
                dve.wait_ge(max_ready, h + 1)
                if not among(h, 0):
                    dve.wait_ge(sc_kept, h * 2)
                dve.tensor_scalar(sc[:, 0:E], DX[:, 0:E], m8[:, 0:1], FLOOR, ALU.subtract, ALU.max).then_inc(sc_ready, 1)

            def best_scores(h):
                dve.wait_ge(sc_ready, h + 1)
                dve.sem_inc(dve_turn, 1)
                dve.max(s8[:], sc[:, 0:E]).then_inc(s8_ready, 1)

            def best_experts(h):
                dve.wait_ge(s8_ready, h + 1)
                dve.sem_inc(dve_turn, 1)
                dve.max_index(i8[:], s8[:], sc[:, 0:E]).then_inc(i8_ready, 1)

            def experts_kept(h):
                dve.wait_ge(i8_ready, h + 1)
                idx = idx_all[:, bass.ds(h, 1), :].rearrange("p a k -> p (a k)")
                dve.tensor_copy(idx, i8[:, 0:K]).then_inc(idx_ready, 1)

            def six_scores(h):
                dve.wait_ge(s8_ready, h + 1)
                dve.tensor_copy(s6[:, 0:K], s8[:, 0:K]).then_inc(s6_ready, 1)

            def experts_marked(h):
                dve.wait_ge(s6_ready, h + 1)
                dve.sem_inc(dve_turn, 1)
                dve.match_replace(marked[:], s6[:], sc[:], MARK).then_inc(marked_ready, 1)

            def experts_mask(h):
                dve.wait_ge(marked_ready, h + 1)
                mk = mask[:, bass.ds(h, 1), :].rearrange("p a e -> p (a e)")
                dve.tensor_scalar(mk, marked[:, 0:E], MARK, None, ALU.is_equal).then_inc(mask_ready, 1)

            def experts_counted(h):
                dve.wait_ge(mask_ready, h + 1)
                dve.tensor_tensor(pre[:, bass.ds(h + 1, 1), :], pre[:, bass.ds(h, 1), :], mask[:, bass.ds(h, 1), :],
                                  ALU.add).then_inc(pre_ready, 1)

            def shared_low(n):
                part, bank = shared_part(n)
                dve.wait_ge(w_sb, n + 2)
                dve.tensor_tensor(part[:, 1, :], bank, part[:, 0, :].bitcast(F32), ALU.subtract).then_inc(sh_lo, 1)

            def iteration(h, s):
                prev, prev2 = not among(h, 0), not among(h, 0, 1)
                nxt, nxt2 = not among(h, NT - 1), not among(h, NT - 2, NT - 1)
                if prev:
                    times(h - 1, 1 - s, 7)
                if prev2:
                    best_logit(h - 2)
                if prev:
                    total(h - 1, 1 - s, 7)
                if prev2:
                    scores(h - 2)
                times(h, s, 0)
                if prev2:
                    best_scores(h - 2)
                times(h, s, 1)
                if prev2:
                    best_experts(h - 2)
                total(h, s, 0)
                if prev2:
                    experts_kept(h - 2)
                if prev:
                    add_x1(h - 1, 1 - s)
                if prev2:
                    six_scores(h - 2)
                total(h, s, 1)
                if prev:
                    stats2(h - 1, 1 - s)
                times(h, s, 2)
                if prev:
                    mean2(h - 1)
                if prev2:
                    experts_marked(h - 2)
                times(h, s, 3)
                if prev:
                    rstd2(h - 1)
                total(h, s, 2)
                if prev:
                    shift2(h - 1)
                last_low_part(h, s)
                if not nxt:
                    shared_low(0)
                total(h, s, 3)
                if prev2:
                    experts_mask(h - 2)
                if nxt:
                    skip_term(h + 1, 1 - s)
                else:
                    shared_low(1)
                times(h, s, 4)
                if prev2:
                    experts_counted(h - 2)
                times(h, s, 5)
                total(h, s, 4)
                if nxt2:
                    rstd1(h + 2)
                if not nxt:
                    shared_low(2)
                total(h, s, 5)
                if nxt2:
                    shift1(h + 2)
                if nxt:
                    filter_low(h + 1, 1 - s)
                    residual(h + 1, 1 - s)
                times(h, s, 6)
                if not nxt:
                    shared_low(3)
                total(h, s, 6)

            for h in range(2):
                rstd1(h)
                shift1(h)
                if h == 0:
                    filter_low(0, 0)
                    skip_term(0, 0)
                    residual(0, 0)
            dve.wait_ge(small_in, 32)
            dve.wait_ge(sc_setup, 2)
            for h in range(3):
                iteration(h, h % 2)
            with dve.Fori(0, 13) as i:
                iteration(i * 2 + 3, 1)
                iteration(i * 2 + 4, 0)
            for h in range(NT - 3, NT):
                iteration(h, h % 2)
            def place_onehot(t):
                idx = idx_all[:, bass.ds(t, 1), :].rearrange("p a k -> p (a k)")
                dve.tensor_tensor(onehot, iota[:].unsqueeze(1).to_broadcast([P, K, E]), idx.unsqueeze(2).to_broadcast([P, K, E]),
                                  ALU.is_equal).then_inc(b_onehot, 1)

            def place_product(t):
                dve.wait_ge(b_onehot, t + 1)
                dve.tensor_tensor(prod, onehot,
                                  pos[:, bass.ds(t, 1), :].to_broadcast([P, K, E]), ALU.mult).then_inc(prod_ready, 1)

            def place_sum(t):
                dve.wait_ge(prod_ready, t + 1)
                dve.tensor_reduce(pk[:], prod, AX.X, ALU.add).then_inc(pk_ready, 1)

            def place_records(t, r):
                dve.wait_ge(pk_ready, t + 1)
                if not among(t, *range(NP)):
                    dve.wait_ge(placed[r], (t - r) * (K * 16 // NP))
                dve.scalar_tensor_tensor(slot[:, r, :], pk[:], float(E), idx_all[:, bass.ds(t, 1), :].rearrange("p a k -> p (a k)"),
                                         ALU.mult, ALU.add).then_inc(slot_ready, 1)
                dve.tensor_copy(recs[:, r, :, :].rearrange("p k c -> p (k c)"),
                                rec[:, bass.ds(t, 1), :, :].rearrange("p a k c -> p (a k c)")).then_inc(slot_ready, 1)

            def place(t, r):
                place_onehot(t)
                place_product(t)
                place_sum(t)
                place_records(t, r)

            def b_rows_low(t, s):
                dve.wait_ge(b_xT_sb, t + 1)
                dve.tensor_tensor(xTs[:, s, 1, :, :].rearrange("p c n -> p (c n)"), TA[:, :],
                                  xTs[:, s, 0, :, :].rearrange("p c n -> p (c n)").bitcast(F32), ALU.subtract).then_inc(b_xT_lo, 1)

            def b_hidden_low(t, s):
                dve.wait_ge(b_hT_sb, t + 1)
                dve.tensor_tensor(hTs[:, s, 1, :, :].rearrange("p c n -> p (c n)"), TB[:, 0:SI],
                                  hTs[:, s, 0, :, :].rearrange("p c n -> p (c n)").bitcast(F32), ALU.subtract).then_inc(b_hT_lo, 1)

            def b_hidden(t, s):
                dve.wait_ge(b_silu, t + 1)
                dve.wait_ge(up_ps, t + 1)
                if not among(t, 0, 1):
                    dve.wait_ge(b_hT_ps, t - 1)
                dve.tensor_tensor(hid[:, s, :], Y[2 * s + 1][:, 0:SI], sg[:, s, :], ALU.mult).then_inc(b_hid, 1)

            def b_result(t, s):
                dve.wait_ge(b_down, t + 1)
                dve.wait_ge(b_x1_in[s], landed(t, s, 16))
                if not among(t, 0, 1):
                    dve.wait_ge(y_out[s], landed(t - 2, s, 16))
                dve.tensor_tensor(y[:, s, :], DN[s][:, :], xr[:, s, :], ALU.add).then_inc(y_ready, 1)

            times(NT - 1, 1, 7)
            best_logit(NT - 2)
            total(NT - 1, 1, 7)
            scores(NT - 2)
            for n in range(4, 7):
                shared_low(n)
            b_rows_low(0, 0)
            shared_low(7)
            add_x1(NT - 1, 1)
            best_scores(NT - 2)
            stats2(NT - 1, 1)
            best_experts(NT - 2)
            mean2(NT - 1)
            experts_kept(NT - 2)
            rstd2(NT - 1)
            six_scores(NT - 2)
            shift2(NT - 1)
            experts_marked(NT - 2)
            shared_low(8)
            experts_mask(NT - 2)
            experts_counted(NT - 2)
            best_logit(NT - 1)
            scores(NT - 1)
            best_scores(NT - 1)
            best_experts(NT - 1)
            experts_kept(NT - 1)
            six_scores(NT - 1)
            experts_marked(NT - 1)
            experts_mask(NT - 1)
            experts_counted(NT - 1)
            b_rows_low(1, 1)
            shared_low(9)
            dve.wait_ge(exp_ready, 3)
            dve.tensor_reduce(sums[:], sc_all[:], AX.X, ALU.add).then_inc(sums_ready, 1)
            dve.wait_ge(sums_ready, 1)
            dve.reciprocal(rinv[:], sums[:]).then_inc(rinv_ready, 1)
            place_onehot(0)
            dve.wait_ge(rinv_ready, 1)
            dve.tensor_tensor(rec[:, :, :, 1], s8_all[:, :, 0:K], rinv[:].unsqueeze(2).to_broadcast([P, NT, K]),
                              ALU.mult).then_inc(rec_ready, 1)
            dve.wait_ge(pos_sb, 1)
            place_product(0)
            b_hidden(0, 0)
            shared_low(10)
            place_sum(0)
            dve.wait_ge(rec_ready, 1)
            place_records(0, 0)
            b_rows_low(2, 0)
            place_onehot(1)
            b_hidden_low(0, 0)
            place_product(1)
            b_hidden(1, 1)
            place_sum(1)
            b_result(0, 0)
            place_records(1, 1)
            dve.wait_ge(pos_sb, 4)

            def b_iteration(t, s, r, ahead=2):
                n = t + ahead
                to_place = not among(t, NT - 2, NT - 1)
                if not among(t, NT - 1):
                    b_rows_low(t + 1, 1 - s)
                if to_place:
                    place_onehot(n)
                b_hidden_low(t - 1, 1 - s)
                if to_place:
                    place_product(n)
                b_hidden(t, s)
                if to_place:
                    place_sum(n)
                b_result(t - 1, 1 - s)
                if to_place:
                    place_records(n, r)

            b_iteration(2, 0, 2, ahead=0)
            place(3, 3)
            b_iteration(3, 1, 0, ahead=1)
            place(5, 1)
            with dve.Fori(1, NT // NP - 1) as i:
                for r in range(NP):
                    b_iteration(i * NP + r, r % 2, (r + 2) % NP)
            for t in range(NT - NP, NT):
                b_iteration(t, t % 2, (t + 2) % NP)
            b_hidden_low(NT - 1, 1)
            b_result(NT - 1, 1)

            dve.wait_ge(table_in, 16)

            def c_hidden(e, s):
                dve.wait_ge(c_silu, e + 1)
                if among(e, 0):
                    dve.wait_ge(b_hT_ps, NT)
                elif not among(e, 1):
                    dve.wait_ge(c_hT_ps, e - 1)
                dve.tensor_tensor(hid[:, s, 0:I], Y[s][:, I:2 * I], sg[:, s, 0:I], ALU.mult).then_inc(c_hid, 1)

            def c_result(e, r):
                s = r % 2
                dve.wait_ge(c_down, e + 1)
                if among(e, 0, 1):
                    dve.wait_ge(y_out[s], NT // 2 * 16)
                elif not among(e, *range(NY)):
                    dve.wait_ge(added, (e - NY + 1) * 16)
                dve.tensor_scalar(eo[r], DN[s][:, :], tbl[:, bass.ds(e, 1), 1], None, ALU.mult).then_inc(eo_ready, 1)

            def c_hidden_low(e, s):
                dve.wait_ge(c_hT_sb, e + 1)
                dve.tensor_tensor(hTs[0:IH, s, 1, 0:2, :].rearrange("p c n -> p (c n)"), TB[0:IH, 0:2 * P],
                                  hTs[0:IH, s, 0, 0:2, :].rearrange("p c n -> p (c n)").bitcast(F32), ALU.subtract).then_inc(c_hT_lo, 1)

            def c_down_low(e, r):
                s = r % 2
                dve.wait_ge(c_d_high, e + 1)
                dve.tensor_tensor(c_d[:, s, 1, :, :].rearrange("p c n -> p (c n)"), ring[0:IH, r, NC * SI:],
                                  c_d[:, s, 0, :, :].rearrange("p c n -> p (c n)").bitcast(F32), ALU.subtract).then_inc(c_d_low, 1)

            def c_iteration(e, r):
                if not among(e, 0):
                    c_hidden_low(e - 1, (r - 1) % 2)
                c_hidden(e, r % 2)
                c_down_low(e, r)
                if not among(e, 0):
                    c_result(e - 1, (r - 1) % NY)

            for e in range(2 * NY):
                c_iteration(e, e % NY)
            with dve.Fori(2, E // NY) as i:
                for r in range(NY):
                    c_iteration(i * NY + r, r)
            c_hidden_low(E - 1, 1)
            c_result(E - 1, (E - 1) % NY)


_INS = ['x', 'fside_S2_0', 'ctx_2048', 'L0_xattn_k', 'L0_ffn_gate_w', 'L0_ffn_gate_up_proj', 'L0_ffn_down_proj',
        'L0_ffn_shared_gate_w', 'L0_ffn_shared_up_w', 'L0_ffn_shared_down_w']


def constants():
    p = np.arange(P)
    b, j = p // NH, p % NH
    sq = np.stack([np.eye(P), b[:, None] == b[None], (b[:, None] == b[None]) & (j[:, None] < j[None]),
                   b[:, None] < b[None]], 1).astype(np.float32)
    iota = np.tile(np.arange(E, dtype=np.float32), (P, 1))
    rec = np.zeros((P, NT, K, 2), np.float32)
    rec[..., 0] = (b * D + j)[:, None, None] + NH * np.arange(NT)[None, :, None]
    table = np.zeros((CAP, E, 2), np.float32)
    table[..., 0] = T + np.arange(CAP)[:, None]
    return {"sq": sq, "iota": iota, "rec": rec.reshape(P, -1), "table": table.reshape(CAP * E, 2)}


def kernel(**inputs):
    import numpy as _np
    import concourse.bacc as _bacc
    from concourse import mybir as _mybir
    from concourse.bass_utils import run_bass_kernel_spmd as _run

    nc = _bacc.Bacc("TRN2", target_bir_lowering=False, num_devices=1)
    arrays, args = {}, []
    data = [(name, inputs[name]) for name in _INS] + list(constants().items())
    for name, value in data:
        a = _np.ascontiguousarray(value)
        arrays[f"in_{name}_dram"] = a
        args.append(nc.dram_tensor(f"in_{name}_dram", a.shape, _mybir.dt.from_np(a.dtype), kind="ExternalInput").ap())
    args.append(nc.dram_tensor("out_0_dram", (T + CAP, L), _mybir.dt.float32, kind="ExternalOutput").ap())
    build(nc, *args)
    r = _run(nc, [arrays], core_ids=[0])
    return r.results[0]["out_0_dram"][:T].reshape(B, D, L)
```
